# Optimizing a Trainium2 kernel written in Bass

```python
import numpy as np
import jax
import jax.numpy as jnp

def _softmax(x, axis=-1):
    return jax.nn.softmax(x, axis=axis)

def _gelu(x):
    return jax.nn.gelu(x, approximate=True)

def _silu(x):
    return jax.nn.silu(x)

def _sigmoid(x):
    return jax.nn.sigmoid(x)

def _layernorm(x, axis=-1, eps=1e-05):
    m = jnp.mean(x, axis=axis, keepdims=True)
    v = jnp.var(x, axis=axis, keepdims=True)
    return (x - m) / jnp.sqrt(v + eps)

def _scatter_add(tgt, idx, src, axis=0):
    return tgt.at[idx].add(src)

def _segment_sum(src, seg, n):
    return jax.ops.segment_sum(src, seg, n)
kernel_name = 'mk_cond_resid_d2_seqx_r2_25264b'

def setup_inputs(seed: int=0):
    np.random.seed(seed)
    _w = jnp.asarray

    def _rec_inputs():
        import jax
        import jax.numpy as jnp
        _rk = jax.random.key(seed)
        x = -7.109e-05 + 0.9999 * jax.random.normal(jax.random.fold_in(_rk, 1), (32, 512, 512), jnp.float32)
        _lenS = 512 - jax.random.randint(jax.random.fold_in(_rk, 7), (32,), 0, max(1, 512 // 4) + 1, jnp.int32)
        _lenS2 = 512 - jax.random.randint(jax.random.fold_in(_rk, 8), (32,), 0, max(1, 512 // 4) + 1, jnp.int32)
        itok_B_0_8 = jax.random.randint(jax.random.fold_in(_rk, 11), (32,), 0, 9, jnp.int32)
        itok_B_0_30 = jax.random.randint(jax.random.fold_in(_rk, 12), (32,), 0, 31, jnp.int32)
        return (x, itok_B_0_8, itok_B_0_30)
    x, itok_B_0_8, itok_B_0_30 = _rec_inputs()

    def _L0_cond_setup():
        import jax, jax.numpy as jnp
        import numpy as np
        LN_EPS = 1e-05
        key = jax.random.key(seed)
        ks = jax.random.split(key, 8)
        B, S, H, A, L = (32, 1024, 512, 128, 10)
        return {'hidden_states': jax.random.normal(ks[0], (B, S, H), dtype=jnp.float32), 'language_ids': jax.random.randint(ks[1], (B,), 0, L, dtype=jnp.int64), 'W1': jax.random.normal(ks[2], (L, H, A), dtype=jnp.float32) * (1.0 / np.sqrt(H)), 'b1': jnp.zeros((L, A), dtype=jnp.float32), 'W2': jax.random.normal(ks[3], (L, A, H), dtype=jnp.float32) * (1.0 / np.sqrt(A)), 'b2': jnp.zeros((L, H), dtype=jnp.float32), 'gamma': jnp.ones((L, H), dtype=jnp.float32), 'beta': jnp.zeros((L, H), dtype=jnp.float32)}
    _L0_cond_all = _L0_cond_setup()
    _L0_cond_in = {k: v for k, v in _L0_cond_all.items() if k in ('W1', 'b1', 'W2', 'b2', 'gamma', 'beta')}
    del _L0_cond_all

    def _L1_cond_setup():
        import jax, jax.numpy as jnp
        import numpy as np
        C, I, O = (32, 512, 512)
        B, T = (64, 256)
        key = jax.random.key(seed)
        kx, kc, kw, kb = jax.random.split(key, 4)
        x = jax.random.normal(kx, (B, T, I), dtype=jnp.float32)
        cat_ids = jax.random.randint(kc, (B,), 0, C)
        W = 0.02 * jax.random.normal(kw, (C, I, O), dtype=jnp.float32)
        b = jnp.zeros((C, O), dtype=jnp.float32)
        return {'x': x, 'cat_ids': cat_ids, 'W': W, 'b': b}
    _L1_cond_all = _L1_cond_setup()
    _L1_cond_in = {k: v for k, v in _L1_cond_all.items() if k in ('W', 'b')}
    del _L1_cond_all
    return {'x': x, 'itok_B_0_8': itok_B_0_8, 'itok_B_0_30': itok_B_0_30, 'L0_cond_W1': _L0_cond_in['W1'], 'L0_cond_b1': _L0_cond_in['b1'], 'L0_cond_W2': _L0_cond_in['W2'], 'L0_cond_b2': _L0_cond_in['b2'], 'L0_cond_gamma': _L0_cond_in['gamma'], 'L0_cond_beta': _L0_cond_in['beta'], 'L1_cond_W': _L1_cond_in['W'], 'L1_cond_b': _L1_cond_in['b']}

def reference(x, itok_B_0_8, itok_B_0_30, L0_cond_W1, L0_cond_b1, L0_cond_W2, L0_cond_b2, L0_cond_gamma, L0_cond_beta, L1_cond_W, L1_cond_b):
    import jax
    import jax.numpy as jnp

    def _L0_cond_ref(hidden_states, language_ids, W1, b1, W2, b2, gamma, beta):
        import jax, jax.numpy as jnp
        import numpy as np
        LN_EPS = 1e-05
        w1 = W1[language_ids]
        w2 = W2[language_ids]
        h = jnp.einsum('bsh,bha->bsa', hidden_states, w1) + b1[language_ids][:, None, :]
        h = jax.nn.relu(h)
        adapted = jnp.einsum('bsa,bah->bsh', h, w2) + b2[language_ids][:, None, :]
        x = hidden_states + adapted
        mean = jnp.mean(x, axis=-1, keepdims=True)
        var = jnp.mean(jnp.square(x - mean), axis=-1, keepdims=True)
        normed = (x - mean) * jax.lax.rsqrt(var + LN_EPS)
        return normed * gamma[language_ids][:, None, :] + beta[language_ids][:, None, :]

    def _L1_cond_ref(x, cat_ids, W, b):
        import jax, jax.numpy as jnp
        import numpy as np
        C, I, O = (32, 512, 512)
        B, T = (64, 256)
        selected_W = W[cat_ids]
        selected_b = b[cat_ids]
        if x.ndim == 2:
            return jnp.einsum('bi,bio->bo', x, selected_W) + selected_b
        return jnp.einsum('bti,bio->bto', x, selected_W) + selected_b[:, None, :]
    x = x + _L0_cond_ref(x, itok_B_0_8, L0_cond_W1, L0_cond_b1, L0_cond_W2, L0_cond_b2, L0_cond_gamma, L0_cond_beta)
    x = x + _L1_cond_ref(x, itok_B_0_30, L1_cond_W, L1_cond_b)
    return x

_drawn_inputs = setup_inputs


def setup_inputs(seed=0):
    import zlib

    import numpy as np

    out = dict(_drawn_inputs(seed))
    spreads = {'L0_cond_b1': (0.0, 0.1),
     'L0_cond_b2': (0.0, 0.1),
     'L0_cond_gamma': (1.0, 0.2),
     'L0_cond_beta': (0.0, 0.1),
     'L1_cond_b': (0.0, 0.1)}
    factors = {}
    for name, (base, spread) in spreads.items():
        noise = np.random.default_rng([zlib.crc32(name.encode()), seed]).standard_normal(out[name].shape)
        drawn = base * np.exp(spread * noise) if base else spread * noise
        out[name] = jnp.asarray(drawn.astype(out[name].dtype))
    for name, factor in factors.items():
        out[name] = (out[name] * factor).astype(out[name].dtype)
    return out
```

```python
import concourse.bass as bass
from concourse import mybir
from contextlib import ExitStack


class Step:

    def __init__(self, h, p):
        self.h, self.p = h, p

    def sample(self, back):
        return 2 * self.h + (self.p - back)

    def pairs(self, back):
        return self.h + (self.p - back) // 2

    def count(self, per, back, more):
        return (2 * per) * self.h + (per * (self.p - back) + more)

    def since(self, k):
        return 2 * self.h + self.p >= k if isinstance(self.h, int) else k <= 2


def adapter_then_conditional_linear(nc, x, lang_ids, cat_ids, W1, b1, W2, b2, gamma, beta, W, b, out):
    F32 = mybir.dt.float32
    F32R = mybir.dt.float32r
    I32 = mybir.dt.int32
    ALU = mybir.AluOpType
    ACT = mybir.ActivationFunctionType

    S, T, H = x.shape
    L, _, A = W1.shape
    G = W.shape[0]
    P = 128
    NT = T // P
    NC = H // P
    NP = 2 * NC + 1
    EPS = 1e-5
    assert A == P and NT == 4 and NC == 4 and S % 2 == 0

    x_rows = x.rearrange("s (p t) h -> s p t h", t=NT)
    out_rows = out.rearrange("s (p t) h -> s p t h", t=NT)
    w1_rows = W1.rearrange("l (c p) a -> l p c a", p=P)
    w_rows = W.rearrange("g (c p) o -> g p c o", p=P)

    ctx = ExitStack()
    with ctx:
        def sb(name, shape, dt=F32):
            return ctx.enter_context(nc.sbuf_tensor(name, shape, dt))

        def bank(name):
            return ctx.enter_context(nc.psum_tensor(name, [P, 512], F32))

        def sem(name):
            return ctx.enter_context(nc.semaphore(name))

        x_tok = [sb(f"x_tok{i}", [P, NT, H]) for i in range(2)]
        w1_raw = [sb(f"w1_raw{i}", [P, NC, A]) for i in range(2)]
        w2_raw = [sb(f"w2_raw{i}", [P, H]) for i in range(2)]
        w_raw = [sb(f"w_raw{i}", [P, NC, H]) for i in range(2)]
        b2_bc = [sb(f"b2_bc{i}", [P, H]) for i in range(2)]
        b_bc = [sb(f"b_bc{i}", [P, H]) for i in range(2)]
        params = [sb(f"params{i}", [P, NP]) for i in range(2)]
        xT_hi = sb("xT_hi", [P, NC, T], F32R)
        xT_lo = sb("xT_lo", [P, NC, T], F32R)
        xT_beta = [sb(f"xT_beta{i}", [P, NC, T]) for i in range(2)]
        w1_hi = [sb(f"w1_hi{i}", [P, NC, A], F32R) for i in range(2)]
        w1_lo = [sb(f"w1_lo{i}", [P, NC, A], F32R) for i in range(2)]
        w2_hi = [sb(f"w2_hi{i}", [P, H], F32R) for i in range(2)]
        w2_lo = [sb(f"w2_lo{i}", [P, H], F32R) for i in range(2)]
        hT_hi = sb("hT_hi", [P, T], F32R)
        hT_lo = sb("hT_lo", [P, T], F32R)
        y = sb("y", [P, NT, H])
        y_sum = sb("y_sum", [P, NT])
        neg_mean = sb("neg_mean", [P, NT])
        sq_sum = sb("sq_sum", [P, NT])
        std = sb("std", [P, NT])
        r0 = sb("r0", [P, NT])
        var_eps = sb("var_eps", [P, NT])
        newton = sb("newton", [P, NT])
        newton2 = sb("newton2", [P, NT])
        rstd = sb("rstd", [P, NT])
        neg_mean_rstd = sb("neg_mean_rstd", [P, NT])
        norm = sb("norm", [P, NT, H])
        x1T_hi = [sb(f"x1T_hi{i}", [P, NC, T], F32R) for i in range(2)]
        x1T_lo = [sb(f"x1T_lo{i}", [P, NC, T], F32R) for i in range(2)]
        w_hi = [sb(f"w_hi{i}", [P, NC, H], F32R) for i in range(2)]
        w_lo = [sb(f"w_lo{i}", [P, NC, H], F32R) for i in range(2)]
        out_half = [sb(f"out_half{i}", [P, NT // 2, H]) for i in range(2)]
        ident = sb("ident", [P, P])
        eps = sb("eps", [P, 1])
        spare = sb("spare", [P, 3])
        ids = sb("ids", [1, 2, S], I32)
        param_rows = sb("param_rows", [L * NP, P])
        param_table = sb("param_table", [P, L, NP])

        x_bank = [bank(f"x_bank{i}") for i in range(2)]
        n_bank = [bank(f"n_bank{i}") for i in range(2)]
        d_bank = [bank(f"d_bank{i}") for i in range(2)]
        down_bank = [d_bank[1], x_bank[0], x_bank[1], d_bank[0]]
        o_bank = [bank(f"o_bank{i}") for i in range(2)]

        setup_in = sem("setup_in")
        x_in = [sem(f"x_in{i}") for i in range(2)]
        adapter_in = [sem(f"adapter_in{i}") for i in range(2)]
        params_in = [sem(f"params_in{i}") for i in range(2)]
        w_in = [sem(f"w_in{i}") for i in range(2)]
        b_in = [sem(f"b_in{i}") for i in range(2)]
        stored = [sem(f"stored{i}") for i in range(2)]
        table_turned = sem("table_turned")
        xT_done = sem("xT_done")
        up_done = sem("up_done")
        down_done = sem("down_done")
        nT_done = sem("nT_done")
        linear_done = sem("linear_done")
        w12_hi_done = sem("w12_hi_done")
        xT_copied = sem("xT_copied")
        norm_act_done = sem("norm_act_done")
        x1_hi_done = sem("x1_hi_done")
        w_hi_done = sem("w_hi_done")
        relu_done = sem("relu_done")
        h_hi_done = sem("h_hi_done")
        sq_done = sem("sq_done")
        std_done = sem("std_done")
        table_done = sem("table_done")
        xT_lo_done = sem("xT_lo_done")
        norm_dve_done = sem("norm_dve_done")
        x1_done = sem("x1_done")
        x1_lo_done = sem("x1_lo_done")
        h_lo_done = sem("h_lo_done")
        y_done = sem("y_done")
        mean_done = sem("mean_done")
        stat_done = sem("stat_done")
        rstd_only_done = sem("rstd_only_done")
        rstd_done = sem("rstd_done")
        out_done = sem("out_done")
        ident_done = sem("ident_done")
        w12_lo_done = sem("w12_lo_done")
        diag_done = sem("diag_done")
        x_b2_done = sem("x_b2_done")
        w_lo_done = sem("w_lo_done")

        OUT_CREDIT = 2
        STORE_CREDIT = 16

        block = ctx.enter_context(nc.Block())

        @block.sync
        def _(sp):
            sp.dma_start(ids[0:1, 0, :], lang_ids.rearrange("(o s) -> o s", o=1)).then_inc(setup_in, 16)
            sp.dma_start(ids[0:1, 1, :], cat_ids.rearrange("(o s) -> o s", o=1)).then_inc(setup_in, 16)

            def sample_id(which, s, count):
                return sp.value_load(ids[0:1, which, bass.ds(s, 1)], min_val=0, max_val=count - 1)

            def load_x(s, p):
                sp.dma_start(x_tok[p][:, :, :], x_rows[bass.ds(s, 1)].rearrange("o p t h -> p (o t) h")
                             ).then_inc(x_in[p], 16)

            def load_adapter(lang, p):
                sp.dma_start(w1_raw[p][:, :, :], w1_rows[bass.ds(lang, 1)].rearrange("o p c a -> p (o c) a")
                             ).then_inc(adapter_in[p], 16)
                sp.dma_start(w2_raw[p][:, :], W2[bass.ds(lang, 1)].rearrange("o a h -> (o a) h")
                             ).then_inc(adapter_in[p], 16)
                sp.dma_start(b2_bc[p][:, :], b2[bass.ds(lang, 1)].to_broadcast([P, H])
                             ).then_inc(adapter_in[p], 16)

            def load_params(lang, p):
                sp.dma_start(params[p][:, :], param_table[:, bass.ds(lang, 1), :].rearrange("p o n -> p (o n)")
                             ).then_inc(params_in[p], 16)

            def load_w(g, p):
                sp.dma_start(w_raw[p][:, :, :], w_rows[bass.ds(g, 1)].rearrange("o p c h -> p (o c) h")
                             ).then_inc(w_in[p], 16)

            def load_b(g, p):
                sp.dma_start(b_bc[p][:, :], b[bass.ds(g, 1)].to_broadcast([P, H])).then_inc(b_in[p], 16)

            def store(k, back, half):
                sp.wait_ge(out_done, k.count(NT, back, 2 * half + 2 + OUT_CREDIT))
                dst = out_rows[bass.ds(k.sample(back), 1)].rearrange("o p t h -> p (o t) h")
                sp.dma_start(dst[:, 2 * half:2 * half + 2, :], out_half[half][:, :, :]
                             ).then_inc(stored[half], 16)

            def step(h, p, loads=True, w_load=True, turn=True, linear=True):
                k, q = Step(h, p), 1 - p
                if w_load:
                    cat_w = sample_id(1, k.sample(0), G)
                if turn:
                    cat_b = sample_id(1, k.sample(1), G)
                if loads:
                    lang = sample_id(0, k.sample(-1), L)
                    if k.since(1):
                        sp.wait_ge(y_done, k.count(NT, 0, 0))
                    load_x(k.sample(-1), q)
                    load_adapter(lang, q)
                if turn:
                    if k.since(2):
                        sp.wait_ge(out_done, k.count(NT, 2, OUT_CREDIT))
                    load_b(cat_b, q)
                if linear:
                    store(k, 2, 0)
                if loads:
                    if k.since(1):
                        sp.wait_ge(x1_done, k.count(NC, 0, 0))
                    load_params(lang, q)
                if w_load:
                    if k.since(2):
                        sp.wait_ge(w_lo_done, k.count(1, 1, 0))
                    load_w(cat_w, p)
                if linear:
                    store(k, 2, 1)

            sp.wait_ge(setup_in, 32)
            lang0 = sample_id(0, 0, L)
            load_x(0, 0)
            load_adapter(lang0, 0)
            for rows, at in ((gamma, 0), (beta, L * NC)):
                sp.dma_start(param_rows[at:at + L * NC, :], rows.rearrange("l (c p) -> (l c) p", p=P)
                             ).then_inc(setup_in, 16)
            sp.dma_start(param_rows[2 * L * NC:L * NP, :], b1).then_inc(setup_in, 16)
            sp.wait_ge(table_done, 3)
            load_params(lang0, 0)

            step(0, 0, turn=False, linear=False)
            step(0, 1, linear=False)
            with sp.Fori(1, S // 2 - 1) as h:
                step(h, 0)
                step(h, 1)
            step(S // 2 - 1, 0)
            step(S // 2 - 1, 1, loads=False)
            for p in range(2):
                step(S // 2, p, loads=False, w_load=False, turn=p == 0)
            for half in range(2):
                sp.wait_ge(stored[half], 16 * S + STORE_CREDIT)

        @block.gpsimd
        def _(pool):
            pool.memset(ident[:, :], 0.0).then_inc(ident_done, 1)
            pool.memset(eps[:, :], EPS).then_inc(ident_done, 1)
            pool.wait_ge(ident_done, 2)
            pool.affine_select(out=ident[:, :], in_=ident[:, :], compare_op=ALU.not_equal, fill=1.0,
                               base=0, pattern=[[-1, P]], channel_multiplier=1).then_inc(ident_done, 1)

            def split_w12(k, back, p):
                pool.wait_ge(w12_hi_done, k.count(2, back, 1))
                pool.tensor_tensor(w1_lo[p][:, :, :], w1_raw[p][:, :, :], w1_hi[p][:, :, :].bitcast(F32),
                                   ALU.subtract).then_inc(w12_lo_done, 1)
                pool.wait_ge(w12_hi_done, k.count(2, back, 2))
                pool.tensor_tensor(w2_lo[p][:, :], w2_raw[p][:, :], w2_hi[p][:, :].bitcast(F32),
                                   ALU.subtract).then_inc(w12_lo_done, 1)

            def step(h, p, adapter=True, turn=True, follow=True):
                k, q = Step(h, p), 1 - p
                if turn:
                    pool.wait_ge(w_in[q], 16 * k.pairs(1) + 16)
                    raw = w_raw[q][:, :, :]
                    blocks = bass.AP(raw.tensor, raw.offset, [[NC * H, P], [H + P, NC], [1, P]])
                    pool.tensor_tensor(blocks, blocks,
                                       ident[:, :].rearrange("p (o n) -> p o n", o=1).to_broadcast([P, NC, P]),
                                       ALU.add).then_inc(diag_done, 1)
                if adapter:
                    pool.wait_ge(xT_done, k.count(NC, 0, NC))
                    for t in range(NT):
                        pool.tensor_tensor(x_tok[p][:, t, :], x_tok[p][:, t, :], b2_bc[p][:, :],
                                           ALU.add).then_inc(x_b2_done, 1)
                if turn:
                    for c in range(NC):
                        pool.wait_ge(w_hi_done, k.count(NC, 1, c + 1))
                        ins = pool.tensor_tensor(w_lo[q][:, c, :], w_raw[q][:, c, :],
                                                 w_hi[q][:, c, :].bitcast(F32), ALU.subtract)
                    ins.then_inc(w_lo_done, 1)
                if follow:
                    split_w12(k, -1, q)

            pool.wait_ge(ident_done, 3)
            split_w12(Step(0, 0), 0, 0)
            step(0, 0, turn=False)
            step(0, 1)
            with pool.Fori(1, S // 2 - 1) as h:
                step(h, 0)
                step(h, 1)
            step(S // 2 - 1, 0)
            step(S // 2 - 1, 1, follow=False)
            step(S // 2, 0, adapter=False, follow=False)

        @block.scalar
        def _(act):
            def split_w12(k, back, p):
                act.wait_ge(adapter_in[p], 48 * k.pairs(back) + 48)
                if k.since(2 + back):
                    act.wait_ge(down_done, k.count(NT, back + 1, 0))
                act.activation(w1_hi[p][:, :, :], w1_raw[p][:, :, :], ACT.Copy).then_inc(w12_hi_done, 1)
                act.activation(w2_hi[p][:, :], w2_raw[p][:, :], ACT.Copy).then_inc(w12_hi_done, 1)

            def step(h, p, adapter=True, turn=True, follow=True):
                k, q = Step(h, p), 1 - p

                def copy_xT(c):
                    act.wait_ge(xT_done, k.count(NC, 0, c + 1))
                    act.activation(xT_hi[:, c, :], x_bank[c % 2][:, :], ACT.Copy)
                    if c == 0:
                        act.wait_ge(params_in[p], 16 * k.pairs(0) + 16)
                    if c == 0 and k.since(2):
                        act.wait_ge(x1_done, k.count(NC, 1, 0))
                    act.activation(xT_beta[p][:, c, :], x_bank[c % 2][:, :], ACT.Identity,
                                   bias=params[p][:, NC + c:NC + c + 1]).then_inc(xT_copied, 1)

                def normalise(t):
                    act.activation(norm[:, t, :], y[:, t, :], ACT.Identity, scale=rstd[:, t:t + 1],
                                   bias=neg_mean_rstd[:, t:t + 1]).then_inc(norm_act_done, 1)

                def x1_hi(c):
                    act.wait_ge(x1_done, k.count(NC, 1, c + 1))
                    act.activation(x1T_hi[q][:, c, :], n_bank[c % 2][:, :], ACT.Copy).then_inc(x1_hi_done, 1)

                if adapter:
                    copy_xT(0)
                    copy_xT(1)
                if turn:
                    act.wait_ge(rstd_done, k.count(1, 0, 0))
                    if k.since(2):
                        act.wait_ge(nT_done, k.count(NC, 1, 0))
                    normalise(0)
                    normalise(1)
                if adapter:
                    copy_xT(2)
                    copy_xT(3)
                if turn:
                    x1_hi(0)
                    x1_hi(1)
                    act.wait_ge(diag_done, k.count(1, 0, 0))
                    for c in range(NC):
                        act.activation(w_hi[q][:, c, :], w_raw[q][:, c, :], ACT.Copy).then_inc(w_hi_done, 1)
                if adapter:
                    act.wait_ge(up_done, k.count(1, 0, 1))
                    act.activation(d_bank[0][:, :], d_bank[0][:, :], ACT.Relu,
                                   bias=params[p][:, 2 * NC:NP]).then_inc(relu_done, 1)
                    act.wait_ge(relu_done, k.count(1, 0, 1))
                    act.activation(hT_hi[:, :], d_bank[0][:, :], ACT.Copy).then_inc(h_hi_done, 1)
                if turn:
                    x1_hi(2)
                    x1_hi(3)
                if follow:
                    split_w12(k, -1, q)
                if adapter:
                    for t in range(NT):
                        act.wait_ge(y_done, k.count(NT, 0, t + 1))
                        if t % 2 == 0:
                            act.wait_ge(mean_done, k.count(2, 0, t // 2 + 1))
                        act.activation(norm[:, t, :], y[:, t, :], ACT.Square, bias=neg_mean[:, t:t + 1],
                                       accum_out=sq_sum[:, t:t + 1]).then_inc(sq_done, 1)
                    act.wait_ge(sq_done, k.count(NT, 0, NT))
                    act.activation(std[:, :], sq_sum[:, :], ACT.Sqrt, scale=1.0 / H,
                                   bias=eps[:, 0:1]).then_inc(std_done, 1)

            act.wait_ge(ident_done, 3)
            split_w12(Step(0, 0), 0, 0)
            step(0, 0, turn=False)
            step(0, 1)
            with act.Fori(1, S // 2 - 1) as h:
                step(h, 0)
                step(h, 1)
            step(S // 2 - 1, 0)
            step(S // 2 - 1, 1, follow=False)
            step(S // 2, 0, adapter=False, follow=False)

        @block.vector
        def _(dve):
            STATS = 4

            dve.memset(spare[:, 0:1], 0.0).then_inc(out_done, OUT_CREDIT)
            for half in range(2):
                dve.memset(spare[:, 1 + half:2 + half], 0.0).then_inc(stored[half], STORE_CREDIT)
            dve.wait_ge(table_turned, 1)
            turned = n_bank[0]
            for at, n, lo in ((0, NC, 0), (L * NC, NC, NC), (2 * L * NC, 1, 2 * NC)):
                dve.tensor_copy(param_table[:, :, lo:lo + n],
                                turned[:, at:at + L * n].rearrange("p (l n) -> p l n", n=n)
                                ).then_inc(table_done, 1)

            def step(h, p, adapter=True, turn=True, linear=True):
                k, q = Step(h, p), 1 - p

                def xT_low(c):
                    dve.wait_ge(xT_copied, k.count(NC, 0, c + 1))
                    dve.tensor_tensor(xT_lo[:, c, :], x_bank[c % 2][:, :], xT_hi[:, c, :].bitcast(F32),
                                      ALU.subtract).then_inc(xT_lo_done, 1)

                def normalise(t):
                    dve.tensor_scalar(norm[:, t, :], y[:, t, :], rstd[:, t:t + 1], neg_mean_rstd[:, t:t + 1],
                                      ALU.mult, ALU.add).then_inc(norm_dve_done, 1)

                def output(t):
                    dve.wait_ge(linear_done, k.count(NT, 2, t + 1))
                    if t == 0:
                        dve.wait_ge(b_in[p], 16 * k.pairs(2) + 16)
                    if t % 2 == 0:
                        dve.wait_ge(stored[t // 2], k.count(16, 2, STORE_CREDIT))
                    dve.tensor_tensor(out_half[t // 2][:, t % 2, :], o_bank[t % 2][:, :], b_bc[p][:, :],
                                      ALU.add).then_inc(out_done, 1)

                def x1(c):
                    dve.wait_ge(nT_done, k.count(NC, 1, c + 1))
                    dve.scalar_tensor_tensor(n_bank[c % 2][:, :], n_bank[c % 2][:, :], params[q][:, c:c + 1],
                                             xT_beta[q][:, c, :], ALU.mult, ALU.add).then_inc(x1_done, 1)

                def x1_low(c):
                    dve.wait_ge(x1_hi_done, k.count(NC, 1, c + 1))
                    dve.tensor_tensor(x1T_lo[q][:, c, :], n_bank[c % 2][:, :], x1T_hi[q][:, c, :].bitcast(F32),
                                      ALU.subtract).then_inc(x1_lo_done, 1)

                def y_tile(t):
                    dve.wait_ge(down_done, k.count(NT, 0, t + 1))
                    dve.wait_ge(x_b2_done, k.count(NT, 0, t + 1))
                    dve.scalar_tensor_tensor(y[:, t, :], down_bank[t][:, :], 1.0, x_tok[p][:, t, :],
                                             ALU.mult, ALU.add, accum_out=y_sum[:, t:t + 1]
                                             ).then_inc(y_done, 1)

                def mean(i):
                    dve.wait_ge(y_done, k.count(NT, 0, 2 * i + 2))
                    dve.tensor_scalar(neg_mean[:, 2 * i:2 * i + 2], y_sum[:, 2 * i:2 * i + 2], -1.0 / H, None,
                                      ALU.mult).then_inc(mean_done, 1)

                if turn:
                    normalise(2)
                    normalise(3)
                if adapter:
                    xT_low(0)
                    xT_low(1)
                if linear:
                    output(0)
                if adapter:
                    xT_low(2)
                    xT_low(3)
                if turn:
                    x1(0)
                    x1(1)
                    x1_low(0)
                    x1_low(1)
                if linear:
                    output(1)
                if turn:
                    x1(2)
                if adapter:
                    dve.wait_ge(h_hi_done, k.count(1, 0, 1))
                    dve.tensor_tensor(hT_lo[:, :], d_bank[0][:, :], hT_hi[:, :].bitcast(F32),
                                      ALU.subtract).then_inc(h_lo_done, 1)
                if turn:
                    x1(3)
                    x1_low(2)
                if adapter:
                    if k.since(1):
                        dve.wait_ge(norm_act_done, k.count(2, 0, 0))
                    y_tile(0)
                    y_tile(1)
                    mean(0)
                    y_tile(2)
                    y_tile(3)
                    mean(1)
                if turn:
                    x1_low(3)
                if linear:
                    output(2)
                if adapter:
                    dve.wait_ge(sq_done, k.count(NT, 0, NT))
                    dve.tensor_scalar(var_eps[:, :], sq_sum[:, :], 1.0 / H, EPS, ALU.mult, ALU.add
                                      ).then_inc(stat_done, 1)
                if linear:
                    output(3)
                if adapter:
                    dve.wait_ge(std_done, k.count(1, 0, 1))
                    dve.reciprocal(r0[:, :], std[:, :]).then_inc(stat_done, 1)
                    dve.wait_ge(stat_done, k.count(STATS, 0, 2))
                    dve.scalar_tensor_tensor(newton[:, :], r0[:, :], -0.5, var_eps[:, :], ALU.mult, ALU.mult
                                             ).then_inc(stat_done, 1)
                    dve.wait_ge(stat_done, k.count(STATS, 0, 3))
                    dve.tensor_tensor(newton2[:, :], newton[:, :], r0[:, :], ALU.mult).then_inc(stat_done, 1)
                    dve.wait_ge(stat_done, k.count(STATS, 0, 4))
                    dve.scalar_tensor_tensor(rstd[:, :], newton2[:, :], 1.5, r0[:, :], ALU.add, ALU.mult
                                             ).then_inc(rstd_only_done, 1)
                    dve.wait_ge(rstd_only_done, k.count(1, 0, 1))
                    dve.tensor_tensor(neg_mean_rstd[:, :], neg_mean[:, :], rstd[:, :], ALU.mult
                                      ).then_inc(rstd_done, 1)
                    dve.wait_ge(rstd_done, k.count(1, 0, 1))

            step(0, 0, turn=False, linear=False)
            step(0, 1, linear=False)
            with dve.Fori(1, S // 2) as h:
                step(h, 0)
                step(h, 1)
            step(S // 2, 0, adapter=False)
            step(S // 2, 1, adapter=False, turn=False)

        @block.tensor
        def _(pe):
            def split_product(acc, lhs_hi, lhs_lo, rhs_hi, rhs_lo, first, last):
                pe.matmul(acc, lhs_hi, rhs_hi, start=first, stop=False)
                pe.matmul(acc, lhs_hi, rhs_lo, start=False, stop=False)
                return pe.matmul(acc, lhs_lo, rhs_hi, start=False, stop=last)

            def step(h, p, adapter=True, turn=True, linear=True):
                k, q = Step(h, p), 1 - p
                first = not k.since(1)

                def turn_x(c):
                    if c == 0:
                        pe.wait_ge(x_in[p], 16 * k.pairs(0) + 16)
                    if c >= 2:
                        pe.wait_ge(xT_lo_done, k.count(NC, 0, c - 1))
                    elif not first:
                        pe.wait_ge(y_done, k.count(NT, 1, c + 2))
                    for t in range(NT):
                        ins = pe.transpose(x_bank[c % 2][:, t * P:(t + 1) * P],
                                           x_tok[p][:, t, c * P:(c + 1) * P], ident[:, :])
                    ins.then_inc(xT_done, 1)

                def turn_norm(c):
                    if c == 0:
                        pe.wait_ge(norm_act_done, k.count(2, 0, 0))
                        pe.wait_ge(norm_dve_done, k.count(2, 0, 0))
                    if k.since(2) or c >= 2:
                        pe.wait_ge(x1_lo_done, k.count(NC, 1, c - 1))
                    for t in range(NT):
                        ins = pe.transpose(n_bank[c % 2][:, t * P:(t + 1) * P],
                                           norm[:, t, c * P:(c + 1) * P], ident[:, :])
                    ins.then_inc(nT_done, 1)

                def up():
                    pe.wait_ge(xT_lo_done, k.count(NC, 0, NC))
                    pe.wait_ge(w12_lo_done, k.count(2, 0, 1))
                    if not first:
                        pe.wait_ge(y_done, k.count(NT, 0, 0))
                    for c in range(NC):
                        ins = split_product(d_bank[0][:, :], w1_hi[p][:, c, :], w1_lo[p][:, c, :],
                                            xT_hi[:, c, :], xT_lo[:, c, :], c == 0, c == NC - 1)
                    ins.then_inc(up_done, 1)

                def down(t):
                    if t == 0:
                        pe.wait_ge(h_lo_done, k.count(1, 0, 1))
                        pe.wait_ge(w12_lo_done, k.count(2, 0, 2))
                    tokens = slice(t * P, (t + 1) * P)
                    split_product(down_bank[t][:, :], hT_hi[:, tokens], hT_lo[:, tokens],
                                  w2_hi[p][:, :], w2_lo[p][:, :], True, True).then_inc(down_done, 1)

                def linear_tile(t):
                    if t == 0:
                        pe.wait_ge(x1_lo_done, k.count(NC, 2, NC))
                        pe.wait_ge(w_lo_done, k.count(1, 1, 0))
                    pe.wait_ge(out_done, k.count(NT, 2, t - 1 + OUT_CREDIT))
                    tokens = slice(t * P, (t + 1) * P)
                    for c in range(NC):
                        ins = split_product(o_bank[t % 2][:, :], x1T_hi[p][:, c, tokens], x1T_lo[p][:, c, tokens],
                                            w_hi[p][:, c, :], w_lo[p][:, c, :], c == 0, c == NC - 1)
                    ins.then_inc(linear_done, 1)

                if adapter:
                    turn_x(0)
                    turn_x(1)
                if linear:
                    linear_tile(0)
                if adapter:
                    turn_x(2)
                    turn_x(3)
                if turn:
                    turn_norm(0)
                    turn_norm(1)
                if linear:
                    linear_tile(1)
                if adapter:
                    up()
                if turn:
                    turn_norm(2)
                    turn_norm(3)
                if linear:
                    linear_tile(2)
                if adapter:
                    for t in range(NT):
                        down(t)
                if linear:
                    linear_tile(3)

            pe.wait_ge(ident_done, 3)
            pe.wait_ge(setup_in, 80)
            pe.transpose(n_bank[0][:, 0:L * NP], param_rows[:, :], ident[0:L * NP, 0:L * NP]
                         ).then_inc(table_turned, 1)
            pe.wait_ge(table_done, 3)
            step(0, 0, turn=False, linear=False)
            step(0, 1, linear=False)
            with pe.Fori(1, S // 2) as h:
                step(h, 0)
                step(h, 1)
            step(S // 2, 0, adapter=False)
            step(S // 2, 1, adapter=False, turn=False)


_INS = ["x", "itok_B_0_8", "itok_B_0_30", "L0_cond_W1", "L0_cond_b1", "L0_cond_W2", "L0_cond_b2",
        "L0_cond_gamma", "L0_cond_beta", "L1_cond_W", "L1_cond_b"]


def kernel(**inputs):
    import numpy as _np
    import concourse.bacc as _bacc
    from concourse import mybir as _mybir
    from concourse.bass_utils import run_bass_kernel_spmd as _run

    nc = _bacc.Bacc("TRN2", target_bir_lowering=False, num_devices=1)
    arrays, args = {}, []
    for name in _INS:
        a = _np.ascontiguousarray(inputs[name])
        arrays[f"in_{name}"] = a
        args.append(nc.dram_tensor(f"in_{name}", a.shape, _mybir.dt.from_np(a.dtype), kind="ExternalInput").ap())
    shape = inputs["x"].shape
    args.append(nc.dram_tensor("out", shape, _mybir.dt.float32, kind="ExternalOutput").ap())
    adapter_then_conditional_linear(nc, *args)
    r = _run(nc, [arrays], core_ids=[0])
    return r.results[0]["out"]
```

```python
import concourse.bass as bass
from concourse import mybir
from contextlib import ExitStack


class Step:

    def __init__(self, h, p):
        self.h, self.p = h, p

    def next(self):
        return Step(self.h + (self.p + 1) // 2, (self.p + 1) % 2)

    def sample(self, back):
        return 2 * self.h + (self.p - back)

    def pairs(self, back):
        return self.h + (self.p - back) // 2

    def count(self, per, back, more):
        return (2 * per) * self.h + (per * (self.p - back) + more)

    def since(self, k):
        return 2 * self.h + self.p >= k if isinstance(self.h, int) else k <= 2


def adapter_then_conditional_linear(nc, x, lang_ids, cat_ids, W1, b1, W2, b2, gamma, beta, W, b, out):
    F32 = mybir.dt.float32
    F32R = mybir.dt.float32r
    I32 = mybir.dt.int32
    ALU = mybir.AluOpType
    ACT = mybir.ActivationFunctionType

    S, T, H = x.shape
    L, _, A = W1.shape
    G = W.shape[0]
    P = 128
    NT = T // P
    NC = H // P
    NP = 2 * NC + 1
    EPS = 1e-5
    assert A == P and NT == 4 and NC == 4 and S % 2 == 0

    x_rows = x.rearrange("s (p t) h -> s p t h", t=NT)
    out_rows = out.rearrange("s (p t) h -> s p t h", t=NT)
    w1_rows = W1.rearrange("l (c p) a -> l p c a", p=P)
    w_rows = W.rearrange("g (c p) o -> g p c o", p=P)

    ctx = ExitStack()
    with ctx:
        def sb(name, shape, dt=F32):
            return ctx.enter_context(nc.sbuf_tensor(name, shape, dt))

        def bank(name):
            return ctx.enter_context(nc.psum_tensor(name, [P, 512], F32))

        def sem(name):
            return ctx.enter_context(nc.semaphore(name))

        x_tok = [sb(f"x_tok{i}", [P, NT, H]) for i in range(2)]
        w1_raw = [sb(f"w1_raw{i}", [P, NC, A]) for i in range(2)]
        w2_raw = [sb(f"w2_raw{i}", [P, H]) for i in range(2)]
        w_raw = [sb(f"w_raw{i}", [P, NC, H]) for i in range(2)]
        b2_bc = [sb(f"b2_bc{i}", [P, H]) for i in range(2)]
        b_bc = [sb(f"b_bc{i}", [P, H]) for i in range(2)]
        params = [sb(f"params{i}", [P, NP]) for i in range(2)]
        xT_hi = sb("xT_hi", [P, NC, T], F32R)
        xT_lo = sb("xT_lo", [P, NC, T], F32R)
        xT_beta = [sb(f"xT_beta{i}", [P, NC, T]) for i in range(2)]
        w1_hi = [sb(f"w1_hi{i}", [P, NC, A], F32R) for i in range(2)]
        w1_lo = [sb(f"w1_lo{i}", [P, NC, A], F32R) for i in range(2)]
        w2_hi = [sb(f"w2_hi{i}", [P, H], F32R) for i in range(2)]
        w2_lo = [sb(f"w2_lo{i}", [P, H], F32R) for i in range(2)]
        hT_hi = sb("hT_hi", [P, T], F32R)
        hT_lo = sb("hT_lo", [P, T], F32R)
        y = sb("y", [P, NT, H])
        y_sum = sb("y_sum", [P, NT])
        neg_mean = sb("neg_mean", [P, NT])
        sq_sum = sb("sq_sum", [P, NT])
        std = sb("std", [P, NT])
        r0 = sb("r0", [P, NT])
        var_eps = sb("var_eps", [P, NT])
        newton = sb("newton", [P, NT])
        newton2 = sb("newton2", [P, NT])
        rstd = sb("rstd", [P, NT])
        neg_mean_rstd = sb("neg_mean_rstd", [P, NT])
        norm = sb("norm", [P, NT, H])
        x1T_hi = [sb(f"x1T_hi{i}", [P, NC, T], F32R) for i in range(2)]
        x1T_lo = [sb(f"x1T_lo{i}", [P, NC, T], F32R) for i in range(2)]
        w_hi = [sb(f"w_hi{i}", [P, NC, H], F32R) for i in range(2)]
        w_lo = [sb(f"w_lo{i}", [P, NC, H], F32R) for i in range(2)]
        out_half = [sb(f"out_half{i}", [P, NT // 2, H]) for i in range(2)]
        ident = sb("ident", [P, P])
        eps = sb("eps", [P, 1])
        zeros = sb("zeros", [P, P])
        spare = sb("spare", [P, 4])
        ids = sb("ids", [1, 2, S], I32)
        param_rows = sb("param_rows", [L * NP, P])
        param_table = sb("param_table", [P, L, NP])

        x_bank = [bank(f"x_bank{i}") for i in range(2)]
        n_bank = [bank(f"n_bank{i}") for i in range(2)]
        d_bank = [bank(f"d_bank{i}") for i in range(2)]
        o_bank = [bank(f"o_bank{i}") for i in range(2)]

        def norm_bank(k, c):
            return [*n_bank, *(n_bank if k.since(2) else o_bank)][c]

        def down_bank(k, t):
            return [d_bank[1], *(x_bank if k.since(1) else o_bank), d_bank[0]][t]

        lang_in = sem("lang_in")
        cat_in = sem("cat_in")
        rows_in = sem("rows_in")
        x0_left_in = sem("x0_left_in")
        x_in = [sem(f"x_in{i}") for i in range(2)]
        adapter_in = [sem(f"adapter_in{i}") for i in range(2)]
        params_in = [sem(f"params_in{i}") for i in range(2)]
        w_in = [sem(f"w_in{i}") for i in range(2)]
        b_in = [sem(f"b_in{i}") for i in range(2)]
        stored = [sem(f"stored{i}") for i in range(2)]
        table_turned = sem("table_turned")
        xT_done = sem("xT_done")
        up_done = sem("up_done")
        down_done = sem("down_done")
        nT_done = sem("nT_done")
        linear_done = sem("linear_done")
        w12_hi_done = sem("w12_hi_done")
        xT_copied = sem("xT_copied")
        norm_act_done = sem("norm_act_done")
        x1_hi_done = sem("x1_hi_done")
        w_hi_done = sem("w_hi_done")
        relu_done = sem("relu_done")
        h_hi_done = sem("h_hi_done")
        sq_done = sem("sq_done")
        std_done = sem("std_done")
        zeros_done = sem("zeros_done")
        first_w12_hi_done = sem("first_w12_hi_done")
        table_done = sem("table_done")
        xT_lo_done = sem("xT_lo_done")
        norm_dve_done = sem("norm_dve_done")
        x1_done = sem("x1_done")
        x1_lo_done = sem("x1_lo_done")
        h_lo_done = sem("h_lo_done")
        y_done = sem("y_done")
        mean_done = sem("mean_done")
        stat_done = sem("stat_done")
        rstd_only_done = sem("rstd_only_done")
        rstd_done = sem("rstd_done")
        out_done = sem("out_done")
        ident_done = sem("ident_done")
        w12_lo_done = sem("w12_lo_done")
        first_beta_done = sem("first_beta_done")
        diag_done = sem("diag_done")
        x_b2_done = sem("x_b2_done")
        w_lo_done = sem("w_lo_done")

        OUT_CREDIT = 2
        STORE_CREDIT = 16

        block = ctx.enter_context(nc.Block())

        @block.sync
        def _(sp):
            def sample_id(which, s, count):
                return sp.value_load(ids[0:1, which, bass.ds(s, 1)], min_val=0, max_val=count - 1)

            def load_x(s, p):
                sp.dma_start(x_tok[p][:, :, :], x_rows[bass.ds(s, 1)].rearrange("o p t h -> p (o t) h")
                             ).then_inc(x_in[p], 16)

            def load_adapter(lang, p):
                sp.dma_start(w1_raw[p][:, :, :], w1_rows[bass.ds(lang, 1)].rearrange("o p c a -> p (o c) a")
                             ).then_inc(adapter_in[p], 16)
                sp.dma_start(w2_raw[p][:, :], W2[bass.ds(lang, 1)].rearrange("o a h -> (o a) h")
                             ).then_inc(adapter_in[p], 16)
                sp.dma_start(b2_bc[p][:, :], b2[bass.ds(lang, 1)].to_broadcast([P, H])
                             ).then_inc(adapter_in[p], 16)

            def load_params(lang, p):
                sp.dma_start(params[p][:, :], param_table[:, bass.ds(lang, 1), :].rearrange("p o n -> p (o n)")
                             ).then_inc(params_in[p], 16)

            def load_w(g, p):
                sp.dma_start(w_raw[p][:, :, :], w_rows[bass.ds(g, 1)].rearrange("o p c h -> p (o c) h")
                             ).then_inc(w_in[p], 16)

            def load_b(g, p):
                sp.dma_start(b_bc[p][:, :], b[bass.ds(g, 1)].to_broadcast([P, H])).then_inc(b_in[p], 16)

            def store(k, back, half, lo=0, hi=2):
                sp.wait_ge(out_done, k.count(NT, back, 2 * half + hi + OUT_CREDIT))
                dst = out_rows[bass.ds(k.sample(back), 1)].rearrange("o p t h -> p (o t) h")
                sp.dma_start(dst[:, 2 * half + lo:2 * half + hi, :], out_half[half][:, lo:hi, :]
                             ).then_inc(stored[half], 16)

            def step(h, p, loads=True, w_load=True, turn=True, linear=True):
                k, q = Step(h, p), 1 - p
                if w_load:
                    cat_w = sample_id(1, k.sample(0), G)
                if turn:
                    cat_b = sample_id(1, k.sample(1), G)
                if loads:
                    lang = sample_id(0, k.sample(-1), L)
                    if k.since(1):
                        sp.wait_ge(y_done, k.count(NT, 0, 0))
                    load_x(k.sample(-1), q)
                    load_adapter(lang, q)
                if turn:
                    if k.since(2):
                        sp.wait_ge(out_done, k.count(NT, 2, OUT_CREDIT))
                    load_b(cat_b, q)
                if linear:
                    store(k, 2, 0)
                if loads:
                    if k.since(1):
                        sp.wait_ge(x1_done, k.count(NC, 0, 0))
                    load_params(lang, q)
                if w_load:
                    if k.since(2):
                        sp.wait_ge(w_lo_done, k.count(1, 1, 0))
                    load_w(cat_w, p)
                if linear:
                    store(k, 2, 1)

            sp.dma_start(ids[0:1, 0, :], lang_ids.rearrange("(o s) -> o s", o=1)).then_inc(lang_in, 16)
            left, right = slice(0, H // 2), slice(H // 2, H)
            sp.dma_start(x_tok[0][:, :, left], x_rows[0, :, :, left]).then_inc(x0_left_in, 16)
            for rows, at in ((gamma, 0), (beta, L * NC)):
                sp.dma_start(param_rows[at:at + L * NC, :], rows.rearrange("l (c p) -> (l c) p", p=P)
                             ).then_inc(rows_in, 16)
            sp.dma_start(param_rows[2 * L * NC:L * NP, :], b1).then_inc(rows_in, 16)
            sp.dma_start(x_tok[0][:, :, right], x_rows[0, :, :, right]).then_inc(x_in[0], 16)
            sp.dma_start(ids[0:1, 1, :], cat_ids.rearrange("(o s) -> o s", o=1)).then_inc(cat_in, 16)
            sp.wait_ge(lang_in, 16)
            lang0 = sample_id(0, 0, L)
            load_adapter(lang0, 0)
            sp.wait_ge(table_done, 3)
            load_params(lang0, 0)
            sp.wait_ge(cat_in, 16)

            step(0, 0, turn=False, linear=False)
            step(0, 1, linear=False)
            with sp.Fori(1, S // 2 - 1) as h:
                step(h, 0)
                step(h, 1)
            step(S // 2 - 1, 0)
            step(S // 2 - 1, 1, loads=False)
            step(S // 2, 0, loads=False, w_load=False)
            last = Step(S // 2, 1)
            store(last, 2, 0)
            store(last, 2, 1, 0, 1)
            store(last, 2, 1, 1, 2)
            sp.wait_ge(stored[0], 16 * S + STORE_CREDIT)
            sp.wait_ge(stored[1], 16 * (S + 1) + STORE_CREDIT)

        @block.gpsimd
        def _(pool):
            pool.memset(ident[:, :], 0.0).then_inc(ident_done, 1)
            pool.memset(eps[:, :], EPS).then_inc(ident_done, 1)
            pool.wait_ge(ident_done, 2)
            pool.affine_select(out=ident[:, :], in_=ident[:, :], compare_op=ALU.not_equal, fill=1.0,
                               base=0, pattern=[[-1, P]], channel_multiplier=1).then_inc(ident_done, 1)

            def split_w12(k, back, p, first=False):
                if first:
                    pool.wait_ge(first_w12_hi_done, 1)
                else:
                    pool.wait_ge(w12_hi_done, k.count(2, back, -1))
                pool.tensor_tensor(w1_lo[p][:, :, :], w1_raw[p][:, :, :], w1_hi[p][:, :, :].bitcast(F32),
                                   ALU.subtract).then_inc(w12_lo_done, 1)
                if first:
                    pool.wait_ge(first_w12_hi_done, 2)
                else:
                    pool.wait_ge(w12_hi_done, k.count(2, back, 0))
                pool.tensor_tensor(w2_lo[p][:, :], w2_raw[p][:, :], w2_hi[p][:, :].bitcast(F32),
                                   ALU.subtract).then_inc(w12_lo_done, 1)

            def step(h, p, adapter=True, turn=True, follow=True):
                k, q = Step(h, p), 1 - p
                if turn:
                    pool.wait_ge(w_in[q], 16 * k.pairs(1) + 16)
                    raw = w_raw[q][:, :, :]
                    blocks = bass.AP(raw.tensor, raw.offset, [[NC * H, P], [H + P, NC], [1, P]])
                    pool.tensor_tensor(blocks, blocks,
                                       ident[:, :].rearrange("p (o n) -> p o n", o=1).to_broadcast([P, NC, P]),
                                       ALU.add).then_inc(diag_done, 1)
                if adapter:
                    pool.wait_ge(xT_done, k.count(NC, 0, NC))
                    for t in range(NT):
                        pool.tensor_tensor(x_tok[p][:, t, :], x_tok[p][:, t, :], b2_bc[p][:, :],
                                           ALU.add).then_inc(x_b2_done, 1)
                if turn:
                    for c in range(NC):
                        pool.wait_ge(w_hi_done, k.count(NC, 1, c + 1))
                        ins = pool.tensor_tensor(w_lo[q][:, c, :], w_raw[q][:, c, :],
                                                 w_hi[q][:, c, :].bitcast(F32), ALU.subtract)
                    ins.then_inc(w_lo_done, 1)
                if follow:
                    split_w12(k, -1, q)

            pool.wait_ge(ident_done, 3)
            split_w12(Step(0, 0), 0, 0, first=True)
            step(0, 0, turn=False)
            step(0, 1)
            with pool.Fori(1, S // 2 - 1) as h:
                step(h, 0)
                step(h, 1)
            step(S // 2 - 1, 0)
            step(S // 2 - 1, 1, follow=False)
            step(S // 2, 0, adapter=False, follow=False)

        @block.scalar
        def _(act):
            def split_w12(k, back, p):
                act.wait_ge(adapter_in[p], 48 * k.pairs(back) + 48)
                if k.since(2 + back):
                    act.wait_ge(down_done, k.count(NT, back + 1, 0))
                act.activation(w1_hi[p][:, :, :], w1_raw[p][:, :, :], ACT.Copy).then_inc(w12_hi_done, 1)
                act.activation(w2_hi[p][:, :], w2_raw[p][:, :], ACT.Copy).then_inc(w12_hi_done, 1)

            def copy_xT(k, c):
                p = k.p
                act.wait_ge(xT_done, k.count(NC, 0, c + 1))
                act.activation(xT_hi[:, c, :], x_bank[c % 2][:, :], ACT.Copy)
                if not k.since(1):
                    act.activation(xT_beta[p][:, c, :], x_bank[c % 2][:, :], ACT.Copy).then_inc(xT_copied, 1)
                    return
                if c == 0:
                    act.wait_ge(params_in[p], 16 * k.pairs(0) + 16)
                if c == 0 and k.since(2):
                    act.wait_ge(x1_done, k.count(NC, 1, 0))
                act.activation(xT_beta[p][:, c, :], x_bank[c % 2][:, :], ACT.Identity,
                               bias=params[p][:, NC + c:NC + c + 1]).then_inc(xT_copied, 1)

            def split_w(k):
                q = 1 - k.p
                act.wait_ge(diag_done, k.count(1, 0, 0))
                for c in range(NC):
                    act.activation(w_hi[q][:, c, :], w_raw[q][:, c, :], ACT.Copy).then_inc(w_hi_done, 1)

            def relu(k):
                act.wait_ge(up_done, k.count(1, 0, 1))
                act.activation(d_bank[0][:, :], d_bank[0][:, :], ACT.Relu,
                               bias=params[k.p][:, 2 * NC:NP]).then_inc(relu_done, 1)
                act.wait_ge(relu_done, k.count(1, 0, 1))
                act.activation(hT_hi[:, :], d_bank[0][:, :], ACT.Copy).then_inc(h_hi_done, 1)

            def step(h, p, adapter=True, turn=True, follow=True):
                k, q = Step(h, p), 1 - p

                def normalise(t):
                    act.activation(norm[:, t, :], y[:, t, :], ACT.Identity, scale=rstd[:, t:t + 1],
                                   bias=neg_mean_rstd[:, t:t + 1]).then_inc(norm_act_done, 1)

                def x1_hi(c):
                    act.wait_ge(x1_done, k.count(NC, 1, c + 1))
                    act.activation(x1T_hi[q][:, c, :], norm_bank(k, c)[:, :], ACT.Copy).then_inc(x1_hi_done, 1)

                if adapter and k.since(2):
                    copy_xT(k, 0)
                    copy_xT(k, 1)
                if turn:
                    act.wait_ge(rstd_done, k.count(1, 0, 0))
                    if k.since(2):
                        act.wait_ge(nT_done, k.count(NC, 1, 0))
                    normalise(0)
                    normalise(1)
                if adapter and k.since(2):
                    copy_xT(k, 2)
                    copy_xT(k, 3)
                if turn and not k.since(2):
                    split_w(k)
                if adapter and not k.since(2):
                    relu(k)
                if not k.since(1):
                    copy_xT(k.next(), 0)
                    copy_xT(k.next(), 1)
                if turn:
                    if k.since(2):
                        split_w(k)
                    x1_hi(0)
                    x1_hi(1)
                if adapter and k.since(2):
                    relu(k)
                if turn:
                    x1_hi(2)
                    x1_hi(3)
                if follow:
                    split_w12(k, -1, q)
                if adapter:
                    for t in range(NT):
                        act.wait_ge(y_done, k.count(NT, 0, t + 1))
                        if t % 2 == 0:
                            act.wait_ge(mean_done, k.count(2, 0, t // 2 + 1))
                        act.activation(norm[:, t, :], y[:, t, :], ACT.Square, bias=neg_mean[:, t:t + 1],
                                       accum_out=sq_sum[:, t:t + 1]).then_inc(sq_done, 1)
                    act.wait_ge(sq_done, k.count(NT, 0, NT))
                    act.activation(std[:, :], sq_sum[:, :], ACT.Sqrt, scale=1.0 / H,
                                   bias=eps[:, 0:1]).then_inc(std_done, 1)
                if not k.since(1):
                    copy_xT(k.next(), 2)
                    copy_xT(k.next(), 3)

            act.wait_ge(ident_done, 2)
            act.activation(spare[:, 3:4], eps[:, :], ACT.Sqrt)
            for c in range(NC):
                copy_xT(Step(0, 0), c)
            act.wait_ge(params_in[0], 16)
            act.wait_ge(xT_copied, NC)
            for c in range(NC):
                act.activation(xT_beta[0][:, c, :], xT_beta[0][:, c, :], ACT.Identity,
                               bias=params[0][:, NC + c:NC + c + 1]).then_inc(first_beta_done, 1)
            step(0, 0, turn=False)
            step(0, 1)
            with act.Fori(1, S // 2 - 1) as h:
                step(h, 0)
                step(h, 1)
            step(S // 2 - 1, 0)
            step(S // 2 - 1, 1, follow=False)
            step(S // 2, 0, adapter=False, follow=False)

        @block.vector
        def _(dve):
            STATS = 4

            dve.memset(zeros[:, :], 0.0).then_inc(zeros_done, 1)
            dve.memset(spare[:, 0:1], 0.0).then_inc(out_done, OUT_CREDIT)
            for half in range(2):
                dve.memset(spare[:, 1 + half:2 + half], 0.0).then_inc(stored[half], STORE_CREDIT)
            dve.wait_ge(table_turned, 1)
            turned = n_bank[0]
            for at, n, lo in ((0, NC, 0), (L * NC, NC, NC), (2 * L * NC, 1, 2 * NC)):
                dve.tensor_copy(param_table[:, :, lo:lo + n],
                                turned[:, at:at + L * n].rearrange("p (l n) -> p l n", n=n)
                                ).then_inc(table_done, 1)

            def xT_low(k, c):
                dve.wait_ge(xT_copied, k.count(NC, 0, c + 1))
                dve.tensor_tensor(xT_lo[:, c, :], x_bank[c % 2][:, :], xT_hi[:, c, :].bitcast(F32),
                                  ALU.subtract).then_inc(xT_lo_done, 1)

            def h_low(k):
                dve.wait_ge(h_hi_done, k.count(1, 0, 1))
                dve.tensor_tensor(hT_lo[:, :], d_bank[0][:, :], hT_hi[:, :].bitcast(F32),
                                  ALU.subtract).then_inc(h_lo_done, 1)

            def step(h, p, adapter=True, turn=True, linear=True):
                k, q = Step(h, p), 1 - p

                def normalise(t):
                    dve.tensor_scalar(norm[:, t, :], y[:, t, :], rstd[:, t:t + 1], neg_mean_rstd[:, t:t + 1],
                                      ALU.mult, ALU.add).then_inc(norm_dve_done, 1)

                def output(t):
                    dve.wait_ge(linear_done, k.count(NT, 2, t + 1))
                    if t == 0:
                        dve.wait_ge(b_in[p], 16 * k.pairs(2) + 16)
                    if t % 2 == 0:
                        dve.wait_ge(stored[t // 2], k.count(16, 2, STORE_CREDIT))
                    dve.tensor_tensor(out_half[t // 2][:, t % 2, :], o_bank[t % 2][:, :], b_bc[p][:, :],
                                      ALU.add).then_inc(out_done, 1)

                def x1(c):
                    dve.wait_ge(nT_done, k.count(NC, 1, c + 1))
                    if not k.since(2):
                        dve.wait_ge(first_beta_done, c + 1)
                    dve.scalar_tensor_tensor(norm_bank(k, c)[:, :], norm_bank(k, c)[:, :], params[q][:, c:c + 1],
                                             xT_beta[q][:, c, :], ALU.mult, ALU.add).then_inc(x1_done, 1)

                def x1_low(c):
                    dve.wait_ge(x1_hi_done, k.count(NC, 1, c + 1))
                    dve.tensor_tensor(x1T_lo[q][:, c, :], norm_bank(k, c)[:, :], x1T_hi[q][:, c, :].bitcast(F32),
                                      ALU.subtract).then_inc(x1_lo_done, 1)

                def y_tile(t):
                    dve.wait_ge(down_done, k.count(NT, 0, t + 1))
                    dve.wait_ge(x_b2_done, k.count(NT, 0, t + 1))
                    dve.scalar_tensor_tensor(y[:, t, :], down_bank(k, t)[:, :], 1.0, x_tok[p][:, t, :],
                                             ALU.mult, ALU.add, accum_out=y_sum[:, t:t + 1]
                                             ).then_inc(y_done, 1)

                def mean(i):
                    dve.wait_ge(y_done, k.count(NT, 0, 2 * i + 2))
                    dve.tensor_scalar(neg_mean[:, 2 * i:2 * i + 2], y_sum[:, 2 * i:2 * i + 2], -1.0 / H, None,
                                      ALU.mult).then_inc(mean_done, 1)

                if adapter and k.since(2):
                    xT_low(k, 0)
                    xT_low(k, 1)
                if turn:
                    normalise(2)
                    normalise(3)
                if linear:
                    output(0)
                if adapter and k.since(2):
                    xT_low(k, 2)
                    xT_low(k, 3)
                if adapter and not k.since(1):
                    h_low(k)
                if turn and not k.since(2):
                    x1(0)
                    h_low(k)
                    x1(1)
                    x1(2)
                    x1(3)
                    y_tile(0)
                    y_tile(1)
                    mean(0)
                    x1_low(0)
                    x1_low(1)
                    y_tile(2)
                    y_tile(3)
                    mean(1)
                    x1_low(2)
                    x1_low(3)
                if linear:
                    output(1)
                if turn and k.since(2):
                    x1(0)
                    x1(1)
                    x1_low(0)
                    x1_low(1)
                if turn and k.since(2):
                    x1(2)
                if adapter and k.since(2):
                    h_low(k)
                if turn and k.since(2):
                    x1(3)
                    x1_low(2)
                if adapter and not (turn and not k.since(2)):
                    if k.since(1):
                        dve.wait_ge(norm_act_done, k.count(2, 0, 0))
                    y_tile(0)
                    y_tile(1)
                    mean(0)
                    if not k.since(1):
                        xT_low(k.next(), 0)
                        xT_low(k.next(), 1)
                    y_tile(2)
                    y_tile(3)
                    mean(1)
                if turn and k.since(2):
                    x1_low(3)
                if linear:
                    output(2)
                if adapter:
                    dve.wait_ge(sq_done, k.count(NT, 0, NT))
                    dve.tensor_scalar(var_eps[:, :], sq_sum[:, :], 1.0 / H, EPS, ALU.mult, ALU.add
                                      ).then_inc(stat_done, 1)
                if linear:
                    output(3)
                if adapter:
                    dve.wait_ge(std_done, k.count(1, 0, 1))
                    dve.reciprocal(r0[:, :], std[:, :]).then_inc(stat_done, 1)
                    dve.wait_ge(stat_done, k.count(STATS, 0, 2))
                    dve.scalar_tensor_tensor(newton[:, :], r0[:, :], -0.5, var_eps[:, :], ALU.mult, ALU.mult
                                             ).then_inc(stat_done, 1)
                    dve.wait_ge(stat_done, k.count(STATS, 0, 3))
                    dve.tensor_tensor(newton2[:, :], newton[:, :], r0[:, :], ALU.mult).then_inc(stat_done, 1)
                    dve.wait_ge(stat_done, k.count(STATS, 0, 4))
                    dve.scalar_tensor_tensor(rstd[:, :], newton2[:, :], 1.5, r0[:, :], ALU.add, ALU.mult
                                             ).then_inc(rstd_only_done, 1)
                    dve.wait_ge(rstd_only_done, k.count(1, 0, 1))
                    dve.tensor_tensor(neg_mean_rstd[:, :], neg_mean[:, :], rstd[:, :], ALU.mult
                                      ).then_inc(rstd_done, 1)
                    dve.wait_ge(rstd_done, k.count(1, 0, 1))
                if not k.since(1):
                    xT_low(k.next(), 2)
                    xT_low(k.next(), 3)

            xT_low(Step(0, 0), 0)
            dve.wait_ge(adapter_in[0], 48)
            dve.tensor_copy(w1_hi[0][:, :, :], w1_raw[0][:, :, :]).then_inc(first_w12_hi_done, 1)
            for c in range(1, NC):
                xT_low(Step(0, 0), c)
            dve.tensor_copy(w2_hi[0][:, :], w2_raw[0][:, :]).then_inc(first_w12_hi_done, 1)
            step(0, 0, turn=False, linear=False)
            step(0, 1, linear=False)
            with dve.Fori(1, S // 2) as h:
                step(h, 0)
                step(h, 1)
            step(S // 2, 0, adapter=False)
            step(S // 2, 1, adapter=False, turn=False)

        @block.tensor
        def _(pe):
            def split_product(acc, lhs_hi, lhs_lo, rhs_hi, rhs_lo, first, last):
                pe.matmul(acc, lhs_hi, rhs_hi, start=first, stop=False)
                pe.matmul(acc, lhs_hi, rhs_lo, start=False, stop=False)
                return pe.matmul(acc, lhs_lo, rhs_hi, start=False, stop=last)

            def keep_clock(count):
                for _ in range(count):
                    pe.matmul(n_bank[1][:, 0:P], zeros[:, :], zeros[:, :], start=True, stop=True)

            def turn_x(k, c):
                if c == 0 and not k.since(1):
                    pe.wait_ge(x0_left_in, 16)
                if c == (0 if k.since(1) else NC // 2):
                    pe.wait_ge(x_in[k.p], 16 * k.pairs(0) + 16)
                if c >= 2:
                    pe.wait_ge(xT_lo_done, k.count(NC, 0, c - 1))
                elif k.since(2):
                    pe.wait_ge(y_done, k.count(NT, 1, c + 2))
                for t in range(NT):
                    ins = pe.transpose(x_bank[c % 2][:, t * P:(t + 1) * P],
                                       x_tok[k.p][:, t, c * P:(c + 1) * P], ident[:, :])
                ins.then_inc(xT_done, 1)

            def step(h, p, adapter=True, turn=True, linear=True):
                k, q = Step(h, p), 1 - p
                first = not k.since(1)

                def turn_norm(c):
                    if c == 0:
                        pe.wait_ge(norm_act_done, k.count(2, 0, 0))
                        pe.wait_ge(norm_dve_done, k.count(2, 0, 0))
                    if k.since(2):
                        pe.wait_ge(x1_lo_done, k.count(NC, 1, c - 1))
                    for t in range(NT):
                        ins = pe.transpose(norm_bank(k, c)[:, t * P:(t + 1) * P],
                                           norm[:, t, c * P:(c + 1) * P], ident[:, :])
                    ins.then_inc(nT_done, 1)

                def up():
                    pe.wait_ge(xT_lo_done, k.count(NC, 0, NC))
                    pe.wait_ge(w12_lo_done, k.count(2, 0, 1))
                    if not first:
                        pe.wait_ge(y_done, k.count(NT, 0, 0))
                    for c in range(NC):
                        ins = split_product(d_bank[0][:, :], w1_hi[p][:, c, :], w1_lo[p][:, c, :],
                                            xT_hi[:, c, :], xT_lo[:, c, :], c == 0, c == NC - 1)
                    ins.then_inc(up_done, 1)

                def down(t):
                    if t == 0:
                        pe.wait_ge(h_lo_done, k.count(1, 0, 1))
                        pe.wait_ge(w12_lo_done, k.count(2, 0, 2))
                    tokens = slice(t * P, (t + 1) * P)
                    split_product(down_bank(k, t)[:, :], hT_hi[:, tokens], hT_lo[:, tokens],
                                  w2_hi[p][:, :], w2_lo[p][:, :], True, True).then_inc(down_done, 1)

                def linear_tile(t):
                    if t == 0:
                        pe.wait_ge(x1_lo_done, k.count(NC, 2, NC))
                        pe.wait_ge(w_lo_done, k.count(1, 1, 0))
                    pe.wait_ge(out_done, k.count(NT, 2, t - 1 + OUT_CREDIT))
                    tokens = slice(t * P, (t + 1) * P)
                    for c in range(NC):
                        ins = split_product(o_bank[t % 2][:, :], x1T_hi[p][:, c, tokens], x1T_lo[p][:, c, tokens],
                                            w_hi[p][:, c, :], w_lo[p][:, c, :], c == 0, c == NC - 1)
                    ins.then_inc(linear_done, 1)

                if adapter and k.since(2):
                    turn_x(k, 0)
                    turn_x(k, 1)
                if linear:
                    linear_tile(0)
                if adapter and k.since(2):
                    turn_x(k, 2)
                    turn_x(k, 3)
                if adapter and not k.since(2):
                    up()
                if linear:
                    linear_tile(1)
                if turn:
                    turn_norm(0)
                    turn_norm(1)
                if first:
                    turn_x(k.next(), 0)
                    turn_x(k.next(), 1)
                    keep_clock(5)
                if adapter and k.since(2):
                    up()
                if turn:
                    turn_norm(2)
                    turn_norm(3)
                if adapter and not k.since(2):
                    for t in range(NT):
                        down(t)
                if linear:
                    linear_tile(2)
                if adapter and k.since(2):
                    for t in range(NT):
                        down(t)
                if first:
                    turn_x(k.next(), 2)
                    turn_x(k.next(), 3)
                    keep_clock(24)
                if linear:
                    linear_tile(3)

            pe.wait_ge(zeros_done, 1)
            keep_clock(9)
            pe.wait_ge(ident_done, 3)
            turn_x(Step(0, 0), 0)
            turn_x(Step(0, 0), 1)
            pe.wait_ge(rows_in, 48)
            pe.transpose(n_bank[0][:, 0:L * NP], param_rows[:, :], ident[0:L * NP, 0:L * NP]
                         ).then_inc(table_turned, 1)
            keep_clock(6)
            turn_x(Step(0, 0), 2)
            keep_clock(4)
            turn_x(Step(0, 0), 3)
            keep_clock(5)
            pe.wait_ge(table_done, 3)
            step(0, 0, turn=False, linear=False)
            step(0, 1, linear=False)
            with pe.Fori(1, S // 2) as h:
                step(h, 0)
                step(h, 1)
            step(S // 2, 0, adapter=False)
            step(S // 2, 1, adapter=False, turn=False)


_INS = ["x", "itok_B_0_8", "itok_B_0_30", "L0_cond_W1", "L0_cond_b1", "L0_cond_W2", "L0_cond_b2",
        "L0_cond_gamma", "L0_cond_beta", "L1_cond_W", "L1_cond_b"]


def kernel(**inputs):
    import numpy as _np
    import concourse.bacc as _bacc
    from concourse import mybir as _mybir
    from concourse.bass_utils import run_bass_kernel_spmd as _run

    nc = _bacc.Bacc("TRN2", target_bir_lowering=False, num_devices=1)
    arrays, args = {}, []
    for name in _INS:
        a = _np.ascontiguousarray(inputs[name])
        arrays[f"in_{name}"] = a
        args.append(nc.dram_tensor(f"in_{name}", a.shape, _mybir.dt.from_np(a.dtype), kind="ExternalInput").ap())
    shape = inputs["x"].shape
    args.append(nc.dram_tensor("out", shape, _mybir.dt.float32, kind="ExternalOutput").ap())
    adapter_then_conditional_linear(nc, *args)
    r = _run(nc, [arrays], core_ids=[0])
    return r.results[0]["out"]
```

```python
import concourse.bass as bass
from concourse import mybir
from contextlib import ExitStack


class Step:

    def __init__(self, h, p):
        self.h, self.p = h, p

    def sample(self, back):
        return 2 * self.h + (self.p - back)

    def pairs(self, back):
        return self.h + (self.p - back) // 2

    def count(self, per, back, more):
        return (2 * per) * self.h + (per * (self.p - back) + more)

    def since(self, k):
        return 2 * self.h + self.p >= k if isinstance(self.h, int) else k <= 2


def adapter_then_conditional_linear(nc, x, lang_ids, cat_ids, W1, b1, W2, b2, gamma, beta, W, b, out):
    F32 = mybir.dt.float32
    F32R = mybir.dt.float32r
    I32 = mybir.dt.int32
    ALU = mybir.AluOpType
    ACT = mybir.ActivationFunctionType

    S, T, H = x.shape
    L, _, A = W1.shape
    G = W.shape[0]
    P = 128
    NT = T // P
    NC = H // P
    NP = 2 * NC + 1
    EPS = 1e-5
    assert A == P and NT == 4 and NC == 4 and S % 2 == 0

    x_rows = x.rearrange("s (p t) h -> s p t h", t=NT)
    out_rows = out.rearrange("s (p t) h -> s p t h", t=NT)
    w1_rows = W1.rearrange("l (c p) a -> l p c a", p=P)
    w_rows = W.rearrange("g (c p) o -> g p c o", p=P)

    ctx = ExitStack()
    with ctx:
        def sb(name, shape, dt=F32):
            return ctx.enter_context(nc.sbuf_tensor(name, shape, dt))

        def bank(name):
            return ctx.enter_context(nc.psum_tensor(name, [P, 512], F32))

        def sem(name):
            return ctx.enter_context(nc.semaphore(name))

        x_tok = [sb(f"x_tok{i}", [P, NT, H]) for i in range(2)]
        w1_raw = [sb(f"w1_raw{i}", [P, NC, A]) for i in range(2)]
        w2_raw = [sb(f"w2_raw{i}", [P, H]) for i in range(2)]
        w_raw = [sb(f"w_raw{i}", [P, NC, H]) for i in range(2)]
        b2_bc = [sb(f"b2_bc{i}", [P, H]) for i in range(2)]
        b_bc = [sb(f"b_bc{i}", [P, H]) for i in range(2)]
        params = [sb(f"params{i}", [P, NP]) for i in range(2)]
        xT_hi = sb("xT_hi", [P, NC, T], F32R)
        xT_lo = sb("xT_lo", [P, NC, T], F32R)
        xT_beta = [sb(f"xT_beta{i}", [P, NC, T]) for i in range(2)]
        w1_hi = [sb(f"w1_hi{i}", [P, NC, A], F32R) for i in range(2)]
        w1_lo = [sb(f"w1_lo{i}", [P, NC, A], F32R) for i in range(2)]
        w2_hi = [sb(f"w2_hi{i}", [P, H], F32R) for i in range(2)]
        w2_lo = [sb(f"w2_lo{i}", [P, H], F32R) for i in range(2)]
        hT_hi = sb("hT_hi", [P, T], F32R)
        hT_lo = sb("hT_lo", [P, T], F32R)
        y = sb("y", [P, NT, H])
        y_sum = sb("y_sum", [P, NT])
        neg_mean = sb("neg_mean", [P, NT])
        sq_sum = sb("sq_sum", [P, NT])
        std = sb("std", [P, NT])
        r0 = sb("r0", [P, NT])
        var_eps = sb("var_eps", [P, NT])
        newton = sb("newton", [P, NT])
        newton2 = sb("newton2", [P, NT])
        rstd = sb("rstd", [P, NT])
        neg_mean_rstd = sb("neg_mean_rstd", [P, NT])
        norm = sb("norm", [P, NT, H])
        x1T_hi = [sb(f"x1T_hi{i}", [P, NC, T], F32R) for i in range(2)]
        x1T_lo = [sb(f"x1T_lo{i}", [P, NC, T], F32R) for i in range(2)]
        w_hi = [sb(f"w_hi{i}", [P, NC, H], F32R) for i in range(2)]
        w_lo = [sb(f"w_lo{i}", [P, NC, H], F32R) for i in range(2)]
        out_half = [sb(f"out_half{i}", [P, NT // 2, H]) for i in range(2)]
        ident = sb("ident", [P, P])
        eps = sb("eps", [P, 1])
        zeros = sb("zeros", [P, P])
        spare = sb("spare", [P, 4])
        ids = sb("ids", [1, 2, S], I32)
        param_rows = sb("param_rows", [L * NP, P])
        param_table = sb("param_table", [P, L, NP])

        x_bank = [bank(f"x_bank{i}") for i in range(2)]
        n_bank = [bank(f"n_bank{i}") for i in range(2)]
        d_bank = [bank(f"d_bank{i}") for i in range(2)]
        o_bank = [bank(f"o_bank{i}") for i in range(2)]

        def xT_bank(k, c):
            return [*x_bank, *(x_bank if k.since(1) else o_bank)][c]

        def norm_bank(k, c):
            return [*n_bank, *(n_bank if k.since(2) else o_bank)][c]

        def down_bank(k, t):
            return [d_bank[1], *(x_bank if k.since(1) else o_bank), d_bank[0]][t]

        lang_in = sem("lang_in")
        cat_in = sem("cat_in")
        rows_in = sem("rows_in")
        x0_left_in = sem("x0_left_in")
        x_in = [sem(f"x_in{i}") for i in range(2)]
        w1_in = [sem(f"w1_in{i}") for i in range(2)]
        w2_in = [sem(f"w2_in{i}") for i in range(2)]
        b2_in = [sem(f"b2_in{i}") for i in range(2)]
        params_in = [sem(f"params_in{i}") for i in range(2)]
        w_in = [sem(f"w_in{i}") for i in range(2)]
        b_in = [sem(f"b_in{i}") for i in range(2)]
        stored = [sem(f"stored{i}") for i in range(2)]
        table_turned = sem("table_turned")
        xT_done = sem("xT_done")
        up_done = sem("up_done")
        down_done = sem("down_done")
        nT_done = sem("nT_done")
        linear_done = sem("linear_done")
        w12_hi_done = sem("w12_hi_done")
        first_xT_hi_done = sem("first_xT_hi_done")
        xT_copied = sem("xT_copied")
        norm_act_done = sem("norm_act_done")
        x1_hi_done = sem("x1_hi_done")
        w_hi_done = sem("w_hi_done")
        relu_done = sem("relu_done")
        h_hi_done = sem("h_hi_done")
        sq_done = sem("sq_done")
        std_done = sem("std_done")
        zeros_done = sem("zeros_done")
        first_w12_hi_done = sem("first_w12_hi_done")
        table_done = sem("table_done")
        xT_lo_done = sem("xT_lo_done")
        norm_dve_done = sem("norm_dve_done")
        x1_done = sem("x1_done")
        x1_lo_done = sem("x1_lo_done")
        h_lo_done = sem("h_lo_done")
        y_done = sem("y_done")
        mean_done = sem("mean_done")
        stat_done = sem("stat_done")
        rstd_only_done = sem("rstd_only_done")
        rstd_done = sem("rstd_done")
        out_done = sem("out_done")
        ident_done = sem("ident_done")
        w12_lo_done = sem("w12_lo_done")
        diag_done = sem("diag_done")
        x_b2_done = sem("x_b2_done")
        w_lo_done = sem("w_lo_done")

        OUT_CREDIT = 2
        STORE_CREDIT = 16

        block = ctx.enter_context(nc.Block())

        @block.sync
        def _(sp):
            def sample_id(which, s, count):
                return sp.value_load(ids[0:1, which, bass.ds(s, 1)], min_val=0, max_val=count - 1)

            def load_x(s, p):
                sp.dma_start(x_tok[p][:, :, :], x_rows[bass.ds(s, 1)].rearrange("o p t h -> p (o t) h")
                             ).then_inc(x_in[p], 16)

            def load_w12(lang, p):
                sp.dma_start(w1_raw[p][:, :, :], w1_rows[bass.ds(lang, 1)].rearrange("o p c a -> p (o c) a")
                             ).then_inc(w1_in[p], 16)
                sp.dma_start(w2_raw[p][:, :], W2[bass.ds(lang, 1)].rearrange("o a h -> (o a) h")
                             ).then_inc(w2_in[p], 16)

            def load_b2(lang, p):
                sp.dma_start(b2_bc[p][:, :], b2[bass.ds(lang, 1)].to_broadcast([P, H])
                             ).then_inc(b2_in[p], 16)

            def load_params(lang, p):
                sp.dma_start(params[p][:, :], param_table[:, bass.ds(lang, 1), :].rearrange("p o n -> p (o n)")
                             ).then_inc(params_in[p], 16)

            def load_w(g, p):
                sp.dma_start(w_raw[p][:, :, :], w_rows[bass.ds(g, 1)].rearrange("o p c h -> p (o c) h")
                             ).then_inc(w_in[p], 16)

            def load_b(g, p):
                sp.dma_start(b_bc[p][:, :], b[bass.ds(g, 1)].to_broadcast([P, H])).then_inc(b_in[p], 16)

            def store(k, back, half, lo=0, hi=2):
                sp.wait_ge(out_done, k.count(NT, back, 2 * half + hi + OUT_CREDIT))
                dst = out_rows[bass.ds(k.sample(back), 1)].rearrange("o p t h -> p (o t) h")
                sp.dma_start(dst[:, 2 * half + lo:2 * half + hi, :], out_half[half][:, lo:hi, :]
                             ).then_inc(stored[half], 16)

            def step(h, p, loads=True, w_load=True, turn=True, linear=True):
                k, q = Step(h, p), 1 - p
                if w_load:
                    cat_w = sample_id(1, k.sample(0), G)
                if turn:
                    cat_b = sample_id(1, k.sample(1), G)
                if loads:
                    lang = sample_id(0, k.sample(-1), L)
                    if k.since(1):
                        sp.wait_ge(y_done, k.count(NT, 0, 0))
                    load_x(k.sample(-1), q)
                    load_w12(lang, q)
                    load_b2(lang, q)
                if turn:
                    if k.since(2):
                        sp.wait_ge(out_done, k.count(NT, 2, OUT_CREDIT))
                    load_b(cat_b, q)
                if linear:
                    store(k, 2, 0)
                if loads:
                    if k.since(1):
                        sp.wait_ge(x1_done, k.count(NC, 0, 0))
                    load_params(lang, q)
                if w_load:
                    if k.since(2):
                        sp.wait_ge(w_lo_done, k.count(1, 1, 0))
                    load_w(cat_w, p)
                if linear:
                    store(k, 2, 1)

            left, right = slice(0, H // 2), slice(H // 2, H)
            sp.dma_start(x_tok[0][:, :, left], x_rows[0, :, :, left]).then_inc(x0_left_in, 16)
            sp.dma_start(ids[0:1, 0, :], lang_ids.rearrange("(o s) -> o s", o=1)).then_inc(lang_in, 16)
            for rows, at in ((gamma, 0), (beta, L * NC)):
                sp.dma_start(param_rows[at:at + L * NC, :], rows.rearrange("l (c p) -> (l c) p", p=P)
                             ).then_inc(rows_in, 16)
            sp.dma_start(param_rows[2 * L * NC:L * NP, :], b1).then_inc(rows_in, 16)
            sp.dma_start(x_tok[0][:, :, right], x_rows[0, :, :, right]).then_inc(x_in[0], 16)
            sp.dma_start(ids[0:1, 1, :], cat_ids.rearrange("(o s) -> o s", o=1)).then_inc(cat_in, 16)
            sp.wait_ge(lang_in, 16)
            lang0 = sample_id(0, 0, L)
            load_w12(lang0, 0)
            sp.wait_ge(table_done, 3)
            load_params(lang0, 0)
            load_b2(lang0, 0)
            sp.wait_ge(cat_in, 16)

            step(0, 0, turn=False, linear=False)
            step(0, 1, linear=False)
            with sp.Fori(1, S // 2 - 1) as h:
                step(h, 0)
                step(h, 1)
            step(S // 2 - 1, 0)
            step(S // 2 - 1, 1, loads=False)
            step(S // 2, 0, loads=False, w_load=False)
            last = Step(S // 2, 1)
            store(last, 2, 0)
            store(last, 2, 1, 0, 1)
            store(last, 2, 1, 1, 2)
            sp.wait_ge(stored[0], 16 * S + STORE_CREDIT)
            sp.wait_ge(stored[1], 16 * (S + 1) + STORE_CREDIT)

        @block.gpsimd
        def _(pool):
            pool.memset(ident[:, :], 0.0).then_inc(ident_done, 1)
            pool.memset(eps[:, :], EPS).then_inc(ident_done, 1)
            pool.wait_ge(ident_done, 2)
            pool.affine_select(out=ident[:, :], in_=ident[:, :], compare_op=ALU.not_equal, fill=1.0,
                               base=0, pattern=[[-1, P]], channel_multiplier=1).then_inc(ident_done, 1)

            def low_w12(p, hi_done, count):
                pool.wait_ge(hi_done, count - 1)
                pool.tensor_tensor(w1_lo[p][:, :, :], w1_raw[p][:, :, :], w1_hi[p][:, :, :].bitcast(F32),
                                   ALU.subtract).then_inc(w12_lo_done, 1)
                pool.wait_ge(hi_done, count)
                pool.tensor_tensor(w2_lo[p][:, :], w2_raw[p][:, :], w2_hi[p][:, :].bitcast(F32),
                                   ALU.subtract).then_inc(w12_lo_done, 1)

            def step(h, p, adapter=True, turn=True, follow=True):
                k, q = Step(h, p), 1 - p
                if turn:
                    pool.wait_ge(w_in[q], 16 * k.pairs(1) + 16)
                    raw = w_raw[q][:, :, :]
                    blocks = bass.AP(raw.tensor, raw.offset, [[NC * H, P], [H + P, NC], [1, P]])
                    pool.tensor_tensor(blocks, blocks,
                                       ident[:, :].rearrange("p (o n) -> p o n", o=1).to_broadcast([P, NC, P]),
                                       ALU.add).then_inc(diag_done, 1)
                if adapter:
                    pool.wait_ge(xT_done, k.count(NC, 0, NC))
                    pool.wait_ge(b2_in[p], 16 * k.pairs(0) + 16)
                    for t in range(NT):
                        pool.tensor_tensor(x_tok[p][:, t, :], x_tok[p][:, t, :], b2_bc[p][:, :],
                                           ALU.add).then_inc(x_b2_done, 1)
                if turn:
                    for c in range(NC):
                        pool.wait_ge(w_hi_done, k.count(NC, 1, c + 1))
                        ins = pool.tensor_tensor(w_lo[q][:, c, :], w_raw[q][:, c, :],
                                                 w_hi[q][:, c, :].bitcast(F32), ALU.subtract)
                    ins.then_inc(w_lo_done, 1)
                if follow:
                    low_w12(q, w12_hi_done, k.count(2, -1, 0))

            pool.wait_ge(ident_done, 3)
            low_w12(0, first_w12_hi_done, 2)
            step(0, 0, turn=False)
            step(0, 1)
            with pool.Fori(1, S // 2 - 1) as h:
                step(h, 0)
                step(h, 1)
            step(S // 2 - 1, 0)
            step(S // 2 - 1, 1, follow=False)
            step(S // 2, 0, adapter=False, follow=False)

        @block.scalar
        def _(act):
            def high_w12_of_next(k):
                q = 1 - k.p
                act.wait_ge(w1_in[q], 16 * k.pairs(-1) + 16)
                if k.since(1):
                    act.wait_ge(down_done, k.count(NT, 0, 0))
                act.activation(w1_hi[q][:, :, :], w1_raw[q][:, :, :], ACT.Copy).then_inc(w12_hi_done, 1)
                act.wait_ge(w2_in[q], 16 * k.pairs(-1) + 16)
                act.activation(w2_hi[q][:, :], w2_raw[q][:, :], ACT.Copy).then_inc(w12_hi_done, 1)

            def xT_plus_beta(k, c):
                if c == 0:
                    act.wait_ge(params_in[k.p], 16 * k.pairs(0) + 16)
                if c == 0 and k.since(2):
                    act.wait_ge(x1_done, k.count(NC, 1, 0))
                act.activation(xT_beta[k.p][:, c, :], xT_bank(k, c)[:, :], ACT.Identity,
                               bias=params[k.p][:, NC + c:NC + c + 1]).then_inc(xT_copied, 1)

            def copy_xT(k, c):
                act.wait_ge(xT_done, k.count(NC, 0, c + 1))
                act.activation(xT_hi[:, c, :], xT_bank(k, c)[:, :], ACT.Copy)
                xT_plus_beta(k, c)

            def normalise(k, t):
                if t == 0:
                    act.wait_ge(rstd_done, k.count(1, 0, 0))
                    if k.since(2):
                        act.wait_ge(nT_done, k.count(NC, 1, 0))
                act.activation(norm[:, t, :], y[:, t, :], ACT.Identity, scale=rstd[:, t:t + 1],
                               bias=neg_mean_rstd[:, t:t + 1]).then_inc(norm_act_done, 1)

            def high_w(k):
                q = 1 - k.p
                act.wait_ge(diag_done, k.count(1, 0, 0))
                for c in range(NC):
                    act.activation(w_hi[q][:, c, :], w_raw[q][:, c, :], ACT.Copy).then_inc(w_hi_done, 1)

            def high_x1(k, c):
                act.wait_ge(x1_done, k.count(NC, 1, c + 1))
                act.activation(x1T_hi[1 - k.p][:, c, :], norm_bank(k, c)[:, :], ACT.Copy).then_inc(x1_hi_done, 1)

            def relu(k):
                act.wait_ge(up_done, k.count(1, 0, 1))
                act.activation(d_bank[0][:, :], d_bank[0][:, :], ACT.Relu,
                               bias=params[k.p][:, 2 * NC:NP]).then_inc(relu_done, 1)
                act.wait_ge(relu_done, k.count(1, 0, 1))
                act.activation(hT_hi[:, :], d_bank[0][:, :], ACT.Copy).then_inc(h_hi_done, 1)

            def deviation(k):
                for t in range(NT):
                    act.wait_ge(y_done, k.count(NT, 0, t + 1))
                    if t % 2 == 0:
                        act.wait_ge(mean_done, k.count(2, 0, t // 2 + 1))
                    act.activation(norm[:, t, :], y[:, t, :], ACT.Square, bias=neg_mean[:, t:t + 1],
                                   accum_out=sq_sum[:, t:t + 1]).then_inc(sq_done, 1)
                act.wait_ge(sq_done, k.count(NT, 0, NT))
                act.activation(std[:, :], sq_sum[:, :], ACT.Sqrt, scale=1.0 / H,
                               bias=eps[:, 0:1]).then_inc(std_done, 1)

            def step(h, p, adapter=True, follow=True):
                k = Step(h, p)
                if adapter:
                    copy_xT(k, 0)
                    copy_xT(k, 1)
                normalise(k, 0)
                normalise(k, 1)
                if adapter:
                    copy_xT(k, 2)
                    copy_xT(k, 3)
                high_w(k)
                high_x1(k, 0)
                high_x1(k, 1)
                if adapter:
                    relu(k)
                high_x1(k, 2)
                high_x1(k, 3)
                if follow:
                    high_w12_of_next(k)
                if adapter:
                    deviation(k)

            act.wait_ge(ident_done, 2)
            act.activation(spare[:, 3:4], eps[:, :], ACT.Sqrt)

            k0, k1 = Step(0, 0), Step(0, 1)
            for c in range(NC):
                act.wait_ge(xT_done, c + 1)
                act.activation(xT_hi[:, c, :], xT_bank(k0, c)[:, :], ACT.Copy).then_inc(first_xT_hi_done, 1)
            for c in range(NC):
                act.wait_ge(xT_lo_done, c + 1)
                xT_plus_beta(k0, c)
            relu(k0)
            copy_xT(k1, 0)
            copy_xT(k1, 1)
            high_w12_of_next(k0)
            deviation(k0)
            copy_xT(k1, 2)
            copy_xT(k1, 3)
            normalise(k1, 0)
            normalise(k1, 1)
            high_w(k1)
            relu(k1)
            for c in range(NC):
                high_x1(k1, c)
            high_w12_of_next(k1)
            deviation(k1)

            with act.Fori(1, S // 2 - 1) as h:
                step(h, 0)
                step(h, 1)
            step(S // 2 - 1, 0)
            step(S // 2 - 1, 1, follow=False)
            step(S // 2, 0, adapter=False, follow=False)

        @block.vector
        def _(dve):
            STATS = 4

            dve.memset(zeros[:, :], 0.0).then_inc(zeros_done, 1)
            dve.memset(spare[:, 0:1], 0.0).then_inc(out_done, OUT_CREDIT)
            for half in range(2):
                dve.memset(spare[:, 1 + half:2 + half], 0.0).then_inc(stored[half], STORE_CREDIT)
            dve.wait_ge(table_turned, 1)
            turned = n_bank[0]
            for at, n, lo in ((0, NC, 0), (L * NC, NC, NC), (2 * L * NC, 1, 2 * NC)):
                dve.tensor_copy(param_table[:, :, lo:lo + n],
                                turned[:, at:at + L * n].rearrange("p (l n) -> p l n", n=n)
                                ).then_inc(table_done, 1)

            def low_xT(k, c):
                if k.since(1):
                    dve.wait_ge(xT_copied, k.count(NC, 0, c + 1))
                else:
                    dve.wait_ge(first_xT_hi_done, c + 1)
                dve.tensor_tensor(xT_lo[:, c, :], xT_bank(k, c)[:, :], xT_hi[:, c, :].bitcast(F32),
                                  ALU.subtract).then_inc(xT_lo_done, 1)

            def low_h(k):
                dve.wait_ge(h_hi_done, k.count(1, 0, 1))
                dve.tensor_tensor(hT_lo[:, :], d_bank[0][:, :], hT_hi[:, :].bitcast(F32),
                                  ALU.subtract).then_inc(h_lo_done, 1)

            def y_pair(k, i):
                if i == 0 and k.since(1):
                    dve.wait_ge(norm_act_done, k.count(2, 0, 0))
                for t in (2 * i, 2 * i + 1):
                    dve.wait_ge(down_done, k.count(NT, 0, t + 1))
                    dve.wait_ge(x_b2_done, k.count(NT, 0, t + 1))
                    dve.scalar_tensor_tensor(y[:, t, :], down_bank(k, t)[:, :], 1.0, x_tok[k.p][:, t, :],
                                             ALU.mult, ALU.add, accum_out=y_sum[:, t:t + 1]
                                             ).then_inc(y_done, 1)
                dve.wait_ge(y_done, k.count(NT, 0, 2 * i + 2))
                dve.tensor_scalar(neg_mean[:, 2 * i:2 * i + 2], y_sum[:, 2 * i:2 * i + 2], -1.0 / H, None,
                                  ALU.mult).then_inc(mean_done, 1)

            def variance(k):
                dve.wait_ge(sq_done, k.count(NT, 0, NT))
                dve.tensor_scalar(var_eps[:, :], sq_sum[:, :], 1.0 / H, EPS, ALU.mult, ALU.add
                                  ).then_inc(stat_done, 1)

            def inverse_deviation(k):
                dve.wait_ge(std_done, k.count(1, 0, 1))
                dve.reciprocal(r0[:, :], std[:, :]).then_inc(stat_done, 1)
                dve.wait_ge(stat_done, k.count(STATS, 0, 2))
                dve.scalar_tensor_tensor(newton[:, :], r0[:, :], -0.5, var_eps[:, :], ALU.mult, ALU.mult
                                         ).then_inc(stat_done, 1)
                dve.wait_ge(stat_done, k.count(STATS, 0, 3))
                dve.tensor_tensor(newton2[:, :], newton[:, :], r0[:, :], ALU.mult).then_inc(stat_done, 1)
                dve.wait_ge(stat_done, k.count(STATS, 0, 4))
                dve.scalar_tensor_tensor(rstd[:, :], newton2[:, :], 1.5, r0[:, :], ALU.add, ALU.mult
                                         ).then_inc(rstd_only_done, 1)
                dve.wait_ge(rstd_only_done, k.count(1, 0, 1))
                dve.tensor_tensor(neg_mean_rstd[:, :], neg_mean[:, :], rstd[:, :], ALU.mult
                                  ).then_inc(rstd_done, 1)
                dve.wait_ge(rstd_done, k.count(1, 0, 1))

            def normalise(k, t):
                dve.tensor_scalar(norm[:, t, :], y[:, t, :], rstd[:, t:t + 1], neg_mean_rstd[:, t:t + 1],
                                  ALU.mult, ALU.add).then_inc(norm_dve_done, 1)

            def x1(k, c):
                q = 1 - k.p
                dve.wait_ge(nT_done, k.count(NC, 1, c + 1))
                dve.scalar_tensor_tensor(norm_bank(k, c)[:, :], norm_bank(k, c)[:, :], params[q][:, c:c + 1],
                                         xT_beta[q][:, c, :], ALU.mult, ALU.add).then_inc(x1_done, 1)

            def low_x1(k, c):
                q = 1 - k.p
                dve.wait_ge(x1_hi_done, k.count(NC, 1, c + 1))
                dve.tensor_tensor(x1T_lo[q][:, c, :], norm_bank(k, c)[:, :], x1T_hi[q][:, c, :].bitcast(F32),
                                  ALU.subtract).then_inc(x1_lo_done, 1)

            def output(k, t):
                dve.wait_ge(linear_done, k.count(NT, 2, t + 1))
                if t == 0:
                    dve.wait_ge(b_in[k.p], 16 * k.pairs(2) + 16)
                if t % 2 == 0:
                    dve.wait_ge(stored[t // 2], k.count(16, 2, STORE_CREDIT))
                dve.tensor_tensor(out_half[t // 2][:, t % 2, :], o_bank[t % 2][:, :], b_bc[k.p][:, :],
                                  ALU.add).then_inc(out_done, 1)

            def step(h, p, adapter=True):
                k = Step(h, p)
                if adapter:
                    low_xT(k, 0)
                    low_xT(k, 1)
                normalise(k, 2)
                normalise(k, 3)
                output(k, 0)
                if adapter:
                    low_xT(k, 2)
                    low_xT(k, 3)
                output(k, 1)
                x1(k, 0)
                x1(k, 1)
                low_x1(k, 0)
                low_x1(k, 1)
                x1(k, 2)
                if adapter:
                    low_h(k)
                x1(k, 3)
                low_x1(k, 2)
                if adapter:
                    y_pair(k, 0)
                    y_pair(k, 1)
                low_x1(k, 3)
                output(k, 2)
                if adapter:
                    variance(k)
                output(k, 3)
                if adapter:
                    inverse_deviation(k)

            k0, k1 = Step(0, 0), Step(0, 1)
            low_xT(k0, 0)
            low_xT(k0, 1)
            dve.wait_ge(w1_in[0], 16)
            dve.tensor_copy(w1_hi[0][:, :, :], w1_raw[0][:, :, :]).then_inc(first_w12_hi_done, 1)
            low_xT(k0, 2)
            low_xT(k0, 3)
            dve.wait_ge(w2_in[0], 16)
            dve.tensor_copy(w2_hi[0][:, :], w2_raw[0][:, :]).then_inc(first_w12_hi_done, 1)
            low_h(k0)
            y_pair(k0, 0)
            y_pair(k0, 1)
            low_xT(k1, 0)
            low_xT(k1, 1)
            variance(k0)
            inverse_deviation(k0)
            low_xT(k1, 2)
            low_xT(k1, 3)
            normalise(k1, 2)
            normalise(k1, 3)
            x1(k1, 0)
            low_h(k1)
            for c in range(1, NC):
                x1(k1, c)
            y_pair(k1, 0)
            low_x1(k1, 0)
            low_x1(k1, 1)
            y_pair(k1, 1)
            low_x1(k1, 2)
            low_x1(k1, 3)
            variance(k1)
            inverse_deviation(k1)

            with dve.Fori(1, S // 2) as h:
                step(h, 0)
                step(h, 1)
            step(S // 2, 0, adapter=False)
            for t in range(NT):
                output(Step(S // 2, 1), t)

        @block.tensor
        def _(pe):
            def split_product(acc, lhs_hi, lhs_lo, rhs_hi, rhs_lo, first, last):
                pe.matmul(acc, lhs_hi, rhs_hi, start=first, stop=False)
                pe.matmul(acc, lhs_hi, rhs_lo, start=False, stop=False)
                return pe.matmul(acc, lhs_lo, rhs_hi, start=False, stop=last)

            def keep_clock(count, idle_bank=n_bank[1]):
                for _ in range(count):
                    pe.matmul(idle_bank[:, 0:P], zeros[:, :], zeros[:, :], start=True, stop=True)

            def turn_x(k, c):
                if not k.since(1):
                    if c == 0:
                        pe.wait_ge(x0_left_in, 16)
                    if c == NC // 2:
                        pe.wait_ge(x_in[0], 16)
                else:
                    if c == 0:
                        pe.wait_ge(x_in[k.p], 16 * k.pairs(0) + 16)
                    if c >= 2:
                        pe.wait_ge(xT_lo_done, k.count(NC, 0, c - 1))
                    elif k.since(2):
                        pe.wait_ge(y_done, k.count(NT, 1, c + 2))
                    elif c == 0:
                        pe.wait_ge(xT_copied, NC)
                for t in range(NT):
                    ins = pe.transpose(xT_bank(k, c)[:, t * P:(t + 1) * P],
                                       x_tok[k.p][:, t, c * P:(c + 1) * P], ident[:, :])
                ins.then_inc(xT_done, 1)

            def turn_norm(k, c):
                if c == 0:
                    pe.wait_ge(norm_act_done, k.count(2, 0, 0))
                    pe.wait_ge(norm_dve_done, k.count(2, 0, 0))
                if k.since(2):
                    pe.wait_ge(x1_lo_done, k.count(NC, 1, c - 1))
                for t in range(NT):
                    ins = pe.transpose(norm_bank(k, c)[:, t * P:(t + 1) * P],
                                       norm[:, t, c * P:(c + 1) * P], ident[:, :])
                ins.then_inc(nT_done, 1)

            def up(k):
                pe.wait_ge(xT_lo_done, k.count(NC, 0, NC))
                pe.wait_ge(w12_lo_done, k.count(2, 0, 1))
                if k.since(1):
                    pe.wait_ge(y_done, k.count(NT, 0, 0))
                for c in range(NC):
                    ins = split_product(d_bank[0][:, :], w1_hi[k.p][:, c, :], w1_lo[k.p][:, c, :],
                                        xT_hi[:, c, :], xT_lo[:, c, :], c == 0, c == NC - 1)
                ins.then_inc(up_done, 1)

            def down(k):
                pe.wait_ge(h_lo_done, k.count(1, 0, 1))
                pe.wait_ge(w12_lo_done, k.count(2, 0, 2))
                for t in range(NT):
                    tokens = slice(t * P, (t + 1) * P)
                    split_product(down_bank(k, t)[:, :], hT_hi[:, tokens], hT_lo[:, tokens],
                                  w2_hi[k.p][:, :], w2_lo[k.p][:, :], True, True).then_inc(down_done, 1)

            def linear_tile(k, t):
                p = k.p
                if t == 0:
                    pe.wait_ge(x1_lo_done, k.count(NC, 2, NC))
                    pe.wait_ge(w_lo_done, k.count(1, 1, 0))
                pe.wait_ge(out_done, k.count(NT, 2, t - 1 + OUT_CREDIT))
                tokens = slice(t * P, (t + 1) * P)
                for c in range(NC):
                    ins = split_product(o_bank[t % 2][:, :], x1T_hi[p][:, c, tokens], x1T_lo[p][:, c, tokens],
                                        w_hi[p][:, c, :], w_lo[p][:, c, :], c == 0, c == NC - 1)
                ins.then_inc(linear_done, 1)

            def step(h, p):
                k = Step(h, p)
                turn_x(k, 0)
                turn_x(k, 1)
                linear_tile(k, 0)
                turn_x(k, 2)
                turn_x(k, 3)
                linear_tile(k, 1)
                turn_norm(k, 0)
                turn_norm(k, 1)
                up(k)
                turn_norm(k, 2)
                turn_norm(k, 3)
                linear_tile(k, 2)
                down(k)
                linear_tile(k, 3)

            k0, k1 = Step(0, 0), Step(0, 1)
            pe.wait_ge(zeros_done, 1)
            keep_clock(8)
            pe.wait_ge(ident_done, 3)
            turn_x(k0, 0)
            pe.wait_ge(rows_in, 48)
            pe.transpose(n_bank[0][:, 0:L * NP], param_rows[:, :], ident[0:L * NP, 0:L * NP]
                         ).then_inc(table_turned, 1)
            turn_x(k0, 1)
            keep_clock(6)
            turn_x(k0, 2)
            turn_x(k0, 3)
            keep_clock(5)
            up(k0)
            turn_x(k1, 0)
            turn_x(k1, 1)
            keep_clock(5)
            down(k0)
            turn_x(k1, 2)
            turn_x(k1, 3)
            keep_clock(14)
            up(k1)
            pe.wait_ge(table_done, 3)
            for c in range(NC):
                turn_norm(k1, c)
            down(k1)
            pe.wait_ge(y_done, NT + 1)
            keep_clock(10, d_bank[1])

            with pe.Fori(1, S // 2) as h:
                step(h, 0)
                step(h, 1)

            k = Step(S // 2, 0)
            linear_tile(k, 0)
            linear_tile(k, 1)
            turn_norm(k, 0)
            turn_norm(k, 1)
            linear_tile(k, 2)
            turn_norm(k, 2)
            turn_norm(k, 3)
            linear_tile(k, 3)
            for t in range(NT):
                linear_tile(Step(S // 2, 1), t)


_INS = ["x", "itok_B_0_8", "itok_B_0_30", "L0_cond_W1", "L0_cond_b1", "L0_cond_W2", "L0_cond_b2",
        "L0_cond_gamma", "L0_cond_beta", "L1_cond_W", "L1_cond_b"]


def kernel(**inputs):
    import numpy as _np
    import concourse.bacc as _bacc
    from concourse import mybir as _mybir
    from concourse.bass_utils import run_bass_kernel_spmd as _run

    nc = _bacc.Bacc("TRN2", target_bir_lowering=False, num_devices=1)
    arrays, args = {}, []
    for name in _INS:
        a = _np.ascontiguousarray(inputs[name])
        arrays[f"in_{name}"] = a
        args.append(nc.dram_tensor(f"in_{name}", a.shape, _mybir.dt.from_np(a.dtype), kind="ExternalInput").ap())
    shape = inputs["x"].shape
    args.append(nc.dram_tensor("out", shape, _mybir.dt.float32, kind="ExternalOutput").ap())
    adapter_then_conditional_linear(nc, *args)
    r = _run(nc, [arrays], core_ids=[0])
    return r.results[0]["out"]
```
